# Optimizing a Trainium2 kernel written in Bass

```python
import numpy as np
import jax
import jax.numpy as jnp

def _softmax(x, axis=-1):
    return jax.nn.softmax(x, axis=axis)

def _gelu(x):
    return jax.nn.gelu(x, approximate=True)

def _silu(x):
    return jax.nn.silu(x)

def _sigmoid(x):
    return jax.nn.sigmoid(x)

def _layernorm(x, axis=-1, eps=1e-05):
    m = jnp.mean(x, axis=axis, keepdims=True)
    v = jnp.var(x, axis=axis, keepdims=True)
    return (x - m) / jnp.sqrt(v + eps)

def _scatter_add(tgt, idx, src, axis=0):
    return tgt.at[idx].add(src)

def _segment_sum(src, seg, n):
    return jax.ops.segment_sum(src, seg, n)
kernel_name = 'mk_adj_resnorm_d2_adj_r2_43287d'

def setup_inputs(seed: int=0):
    np.random.seed(seed)
    _w = jnp.asarray

    def _rec_inputs():
        import jax
        import jax.numpy as jnp
        _gk = jax.random.key(seed)
        x = 7.22e-05 + 1 * jax.random.normal(jax.random.fold_in(_gk, 1), (64, 128, 256), jnp.float32)
        _a = jax.random.bernoulli(jax.random.fold_in(_gk, 2), 0.015625, (128, 128))
        _a = jnp.logical_or(_a, jnp.swapaxes(_a, -1, -2))
        _a = jnp.logical_or(_a, jnp.eye(128, dtype=bool))
        _af = _a.astype(jnp.float32)
        adj = _af
        return (x, adj)
    x, adj = _rec_inputs()

    def _L0_gnn_setup():
        import jax, jax.numpy as jnp
        import numpy as np
        B, N, D = (8, 1024, 256)
        key = jax.random.key(seed)
        k1, k2, k3, k4, k5 = jax.random.split(key, 5)
        neuron_states = jax.random.normal(k1, (B, N, D), dtype=jnp.float32)
        adjacency = jax.random.randint(k2, (N, N), 0, 2).astype(jnp.float32)
        scale = 1.0 / np.sqrt(D)
        Wq = jax.random.normal(k3, (D, D), dtype=jnp.float32) * scale
        Wk = jax.random.normal(k4, (D, D), dtype=jnp.float32) * scale
        Wv = jax.random.normal(k5, (D, D), dtype=jnp.float32) * scale
        return {'neuron_states': neuron_states, 'adjacency': adjacency, 'Wq': Wq, 'Wk': Wk, 'Wv': Wv}
    _L0_gnn_all = _L0_gnn_setup()
    _L0_gnn_in = {k: v for k, v in _L0_gnn_all.items() if k in ('Wq', 'Wk', 'Wv')}
    del _L0_gnn_all

    def _L1_gnn_setup():
        import jax, jax.numpy as jnp
        import numpy as np
        B, N, D, H = (16, 1025, 256, 8)
        LN_EPS = 1e-05

        def _make_mask(key, n):
            n_proto = n - 1
            adj = jax.random.bernoulli(key, 0.03, (n_proto, n_proto)).astype(jnp.float32)
            adj = jnp.clip(adj + adj.T + jnp.eye(n_proto, dtype=jnp.float32), 0.0, 1.0)
            mask = jnp.zeros((n, n), dtype=jnp.float32)
            mask = mask.at[0, :].set(1.0).at[:, 0].set(1.0)
            mask = mask.at[1:, 1:].set(adj)
            return mask
        key = jax.random.key(seed)
        ks = jax.random.split(key, 7)
        s = 1.0 / np.sqrt(D)
        return {'x': jax.random.normal(ks[0], (B, N, D), dtype=jnp.float32), 'w_qkv': jax.random.uniform(ks[1], (D, 3 * D), dtype=jnp.float32, minval=-s, maxval=s), 'w_proj': jax.random.uniform(ks[2], (D, D), dtype=jnp.float32, minval=-s, maxval=s), 'b_proj': jnp.zeros((D,), dtype=jnp.float32), 'ln_gamma': jnp.ones((D,), dtype=jnp.float32), 'ln_beta': jnp.zeros((D,), dtype=jnp.float32), 'attn_mask': _make_mask(ks[3], N)}
    _L1_gnn_all = _L1_gnn_setup()
    _L1_gnn_in = {k: v for k, v in _L1_gnn_all.items() if k in ('w_qkv', 'w_proj', 'b_proj', 'ln_gamma', 'ln_beta')}
    del _L1_gnn_all
    return {'x': x, 'adj': adj, 'L0_gnn_Wq': _L0_gnn_in['Wq'], 'L0_gnn_Wk': _L0_gnn_in['Wk'], 'L0_gnn_Wv': _L0_gnn_in['Wv'], 'L1_gnn_w_qkv': _L1_gnn_in['w_qkv'], 'L1_gnn_w_proj': _L1_gnn_in['w_proj'], 'L1_gnn_b_proj': _L1_gnn_in['b_proj'], 'L1_gnn_ln_gamma': _L1_gnn_in['ln_gamma'], 'L1_gnn_ln_beta': _L1_gnn_in['ln_beta']}

def reference(x, adj, L0_gnn_Wq, L0_gnn_Wk, L0_gnn_Wv, L1_gnn_w_qkv, L1_gnn_w_proj, L1_gnn_b_proj, L1_gnn_ln_gamma, L1_gnn_ln_beta):
    import jax
    import jax.numpy as jnp

    def _L0_gnn_ref(neuron_states, adjacency, Wq, Wk, Wv):
        import jax, jax.numpy as jnp
        import numpy as np
        B, N, D = (8, 1024, 256)
        q = jnp.einsum('bnd,ed->bne', neuron_states, Wq)
        k = jnp.einsum('bnd,ed->bne', neuron_states, Wk)
        v = jnp.einsum('bnd,ed->bne', neuron_states, Wv)
        rel = jnp.einsum('bnd,bmd->bnm', q, k)
        rel = adjacency.T[None, :, :] * rel
        rel = rel / jnp.linalg.norm(rel, axis=2, keepdims=True)
        return jnp.einsum('bnm,bmd->bnd', rel, v)

    def _L1_gnn_ref(x, w_qkv, w_proj, b_proj, ln_gamma, ln_beta, attn_mask):
        import jax, jax.numpy as jnp
        import numpy as np
        B, N, D, H = (16, 1025, 256, 8)
        LN_EPS = 1e-05

        def _make_mask(key, n):
            n_proto = n - 1
            adj = jax.random.bernoulli(key, 0.03, (n_proto, n_proto)).astype(jnp.float32)
            adj = jnp.clip(adj + adj.T + jnp.eye(n_proto, dtype=jnp.float32), 0.0, 1.0)
            mask = jnp.zeros((n, n), dtype=jnp.float32)
            mask = mask.at[0, :].set(1.0).at[:, 0].set(1.0)
            mask = mask.at[1:, 1:].set(adj)
            return mask
        b, n, d = x.shape
        hd = d // H
        scale = hd ** (-0.5)
        qkv = (x @ w_qkv).reshape(b, n, 3, H, hd).transpose(2, 0, 3, 1, 4)
        q, k, v = (qkv[0], qkv[1], qkv[2])
        attn = jnp.einsum('bhnd,bhmd->bhnm', q, k) * scale
        attn = jnp.where(attn_mask[None, None] == 0, -jnp.inf, attn)
        attn = jax.nn.softmax(attn, axis=-1)
        o = jnp.einsum('bhnm,bhmd->bhnd', attn, v).transpose(0, 2, 1, 3).reshape(b, n, d)
        o = o @ w_proj + b_proj
        mu = jnp.mean(o, axis=-1, keepdims=True)
        var = jnp.mean(jnp.square(o - mu), axis=-1, keepdims=True)
        ln = (o - mu) * jax.lax.rsqrt(var + LN_EPS) * ln_gamma + ln_beta
        return o + ln
    x = _layernorm(x + _L0_gnn_ref(x, adj, L0_gnn_Wq, L0_gnn_Wk, L0_gnn_Wv), axis=-1)
    x = _layernorm(x + _L1_gnn_ref(x, L1_gnn_w_qkv, L1_gnn_w_proj, L1_gnn_b_proj, L1_gnn_ln_gamma, L1_gnn_ln_beta, adj), axis=-1)
    return x

_drawn_inputs = setup_inputs


def setup_inputs(seed=0):
    import zlib

    import numpy as np

    out = dict(_drawn_inputs(seed))
    spreads = {'L1_gnn_b_proj': (0.0, 0.1), 'L1_gnn_ln_gamma': (1.0, 0.2), 'L1_gnn_ln_beta': (0.0, 0.1)}
    factors = {}
    for name, (base, spread) in spreads.items():
        noise = np.random.default_rng([zlib.crc32(name.encode()), seed]).standard_normal(out[name].shape)
        drawn = base * np.exp(spread * noise) if base else spread * noise
        out[name] = jnp.asarray(drawn.astype(out[name].dtype))
    for name, factor in factors.items():
        out[name] = (out[name] * factor).astype(out[name].dtype)
    return out
```

```python
import concourse.bass as bass
from concourse import mybir
from contextlib import ExitStack


def gnn_two_layer_kernel(nc, x, adj, wq0, wk0, wv0, w_qkv, w_proj, b_proj, gamma, beta, out):
    fp32 = mybir.dt.float32
    f32r = mybir.dt.float32r
    bf16 = mybir.dt.bfloat16
    ALU = mybir.AluOpType
    ACT = mybir.ActivationFunctionType
    AX = mybir.AxisListType

    BATCH, N, D = x.shape
    H = 8
    HD = D // H
    S = 2
    C = D // 128
    R = 128 // HD
    J = S * C
    PAIRS = BATCH // S
    HALF = C * S * N // 2
    EPS = 1e-5
    SCALE = float(HD) ** -0.5
    MASKED = -1e30
    LOOP_FROM, LOOP_TO = 4, PAIRS - 2

    x_pairs = x.rearrange("(p s) n d -> p n s d", s=S)
    out_pairs = out.rearrange("(p s) n d -> p n s d", s=S)

    ctx = ExitStack()
    with ctx:
        def sb(name, shape, dt=fp32):
            return ctx.enter_context(nc.sbuf_tensor(name, shape, dt))

        def sem(name):
            return ctx.enter_context(nc.semaphore(name))

        wq0_sb = sb("wq0_sb", [128, C, D])
        wk0_sb = sb("wk0_sb", [128, C, D])
        wv0_sb = sb("wv0_sb", [128, C, D])
        wqkv_sb = sb("wqkv_sb", [128, C, 3 * D])
        wproj_sb = sb("wproj_sb", [128, C, D])
        adj_sb = sb("adj_sb", [N, N])
        bias_bc = sb("bias_bc", [128, D])
        bias2 = sb("bias2", [128, S, D])
        gamma_bc = sb("gamma_bc", [128, D])
        beta_bc = sb("beta_bc", [128, D])
        beta2 = sb("beta2", [128, S, D])
        ident = sb("ident", [128, 128])
        ident_bf = sb("ident_bf", [128, 128], bf16)
        mask_bf = sb("mask_bf", [N, J, N], bf16)
        eps_c = sb("eps_c", [128, S])
        mhalf_c = sb("mhalf_c", [128, S])
        m_hi = sb("m_hi", [128, C, D], f32r)
        m_lo = sb("m_lo", [128, C, D], f32r)
        wu_hi = sb("wu_hi", [128, C, S, D + N], f32r)
        wu_lo = sb("wu_lo", [128, C, S, D + N], f32r)
        wqk_hi = sb("wqk_hi", [128, C, 2 * D], f32r)
        wqk_lo = sb("wqk_lo", [128, C, 2 * D], f32r)
        wv1_hi = sb("wv1_hi", [128, C, D], f32r)
        wv1_lo = sb("wv1_lo", [128, C, D], f32r)
        wp_hi = sb("wp_hi", [128, C, D], f32r)
        wp_lo = sb("wp_lo", [128, C, D], f32r)

        x_sb = [sb(f"x_sb{b}", [N, S, D]) for b in range(2)]
        xT_hi = sb("xT_hi", [128, C, S, N], f32r)
        xT_lo = sb("xT_lo", [128, C, S, N], f32r)
        v0_sb = sb("v0_sb", [N, S, D])
        relm = sb("relm", [N, S, N])
        sq_junk = sb("sq_junk", [N, S, N])
        ssq = sb("ssq", [N, S])
        rnorm = sb("rnorm", [N, S])
        y0 = sb("y0", [N, S, D])
        st0 = sb("st0", [N, S, 6])
        mv0 = sb("mv0", [N, S, 2])
        ve0 = sb("ve0", [N, S])
        rstd0 = sb("rstd0", [N, S])
        x1 = [sb(f"x1_{b}", [N, S, D]) for b in range(2)]
        x1b = [sb(f"x1b_{b}", [N, S, D]) for b in range(2)]
        x1T_hi = sb("x1T_hi", [128, C, S, N], f32r)
        x1T_lo = sb("x1T_lo", [128, C, S, N], f32r)
        qT = sb("qT", [128, C, S, N])
        kT = sb("kT", [128, C, S, N])
        v1 = [sb(f"v1_{b}", [N, S, D]) for b in range(2)]
        nmax = sb("nmax", [N, R, J])
        rsum = sb("rsum", [N, R, J])
        rinv = sb("rinv", [N, R, J])
        prob = [sb(f"prob{b}", [N, R, J, N]) for b in range(2)]
        pT = sb("pT", [N, R, J, N])
        oT_hi = sb("oT_hi", [128, S, C, N], f32r)
        oT_lo = sb("oT_lo", [128, S, C, N], f32r)
        o_sb = sb("o_sb", [N, S, D])
        ores = sb("ores", [N, S, D])
        og = sb("og", [N, S, D])
        y1 = sb("y1", [N, S, D])
        st1 = sb("st1", [N, S, 6])
        mv1 = sb("mv1", [N, S, 2])
        ve1 = sb("ve1", [N, S])
        rstd1 = sb("rstd1", [N, S])
        st2 = sb("st2", [N, S, 6])
        mv2 = sb("mv2", [N, S, 2])
        ve2 = sb("ve2", [N, S])
        rstd2 = sb("rstd2", [N, S])
        x2 = [sb(f"x2_{b}", [N, S, D]) for b in range(2)]

        score = [ctx.enter_context(nc.psum_tensor(f"score{r}", [128, J, N], fp32)) for r in range(R)]
        work = [ctx.enter_context(nc.psum_tensor(f"work{b}", [128, 512], fp32)) for b in range(4)]
        u_bank = work[0]
        pt01_bank = [work[1], work[2]]
        vr_bank = [work[3], work[0]]
        rt_bank, o0_bank = work[1], work[2]
        pt23_bank = [work[3], work[0]]
        ot_bank, x1T_bank, pr_bank = work[1], work[2], work[3]
        q_bank, k_bank, v1_bank, xT_bank = work[0], work[1], work[2], work[3]

        weights_loaded = sem("weights_loaded")
        ident_zeroed = sem("ident_zeroed")
        ident_ready = sem("ident_ready")
        pool_consts = sem("pool_consts")
        m_made = sem("m_made")
        wvT_made = sem("wvT_made")
        setup_step = sem("setup_step")
        setup_done = sem("setup_done")
        x_loaded = [sem(f"x_loaded{b}") for b in range(2)]
        x2_stored = [sem(f"x2_stored{b}") for b in range(2)]
        xT_made = sem("xT_made")
        u_made = sem("u_made")
        vr_made = [sem(f"vr_made{s}") for s in range(S)]
        rel_made = sem("rel_made")
        o0_made = sem("o0_made")
        x1T_made = sem("x1T_made")
        q_made = sem("q_made")
        k_made = sem("k_made")
        v1_made = sem("v1_made")
        scores_made = sem("scores_made")
        pT_made = [sem(f"pT_made{r}") for r in range(R)]
        oT_made = sem("oT_made")
        pr_made = sem("pr_made")
        xT_hi_done = sem("xT_hi_done")
        u_hi_done = sem("u_hi_done")
        v0_done = [sem(f"v0_done{s}") for s in range(S)]
        ssq_done = sem("ssq_done")
        x1T_hi_done = sem("x1T_hi_done")
        q_done = sem("q_done")
        k_done = sem("k_done")
        v1_done = sem("v1_done")
        exp_done = [sem(f"exp_done{r}") for r in range(R)]
        pT_done = [sem(f"pT_done{r}") for r in range(R)]
        oT_hi_done = sem("oT_hi_done")
        xT_lo_done = sem("xT_lo_done")
        u_lo_done = sem("u_lo_done")
        relm_done = [sem(f"relm_done{s}") for s in range(S)]
        y0_done = sem("y0_done")
        st0_done = sem("st0_done")
        mv0_done = sem("mv0_done")
        x1_done = sem("x1_done")
        x1T_lo_done = sem("x1T_lo_done")
        max_done = [sem(f"max_done{r}") for r in range(R)]
        rinv_done = [sem(f"rinv_done{r}") for r in range(R)]
        oT_lo_done = sem("oT_lo_done")
        o_done = sem("o_done")
        st1_done = sem("st1_done")
        mv1_done = sem("mv1_done")
        og_done = sem("og_done")
        y1_done = sem("y1_done")
        st2_done = sem("st2_done")
        mv2_done = sem("mv2_done")
        x2_done = sem("x2_done")
        rnorm_done = sem("rnorm_done")
        ve0_done = sem("ve0_done")
        rstd0_done = sem("rstd0_done")
        x1b_done = sem("x1b_done")
        prob_done = [sem(f"prob_done{r}") for r in range(R)]
        ores_done = sem("ores_done")
        ve1_done = sem("ve1_done")
        rstd1_done = sem("rstd1_done")
        ve2_done = sem("ve2_done")
        rstd2_done = sem("rstd2_done")

        def wait(eng, semaphore, count):
            if not (isinstance(count, int) and count <= 0):
                eng.wait_ge(semaphore, count)

        def counts(eng, t):
            kept = {}

            def count(c):
                if isinstance(t, int):
                    return min(t + c, PAIRS)
                if c not in kept:
                    kept[c] = eng.snap(t + c)
                return kept[c]
            return count

        def dma_count(eng, t, c, b):
            if isinstance(t, int):
                return 8 * (t + c - b) + 16
            return eng.snap(8 * t + (8 * (c - b) + 16))

        def run_steps(eng, step):
            for t in range(LOOP_FROM):
                step(t, t % 2)
            with eng.Fori(LOOP_FROM, LOOP_TO - 1, 2) as t:
                step(t, 0)
                step(t + 1, 1)
            for t in range(LOOP_TO, PAIRS + 2):
                step(t, t % 2)

        def present(t, c):
            return not isinstance(t, int) or 0 <= t + c < PAIRS

        block = ctx.enter_context(nc.Block())

        @block.sync
        def _(sp):
            for dst, src in ((adj_sb, adj),
                             (wq0_sb, wq0.rearrange("(c p) n -> p c n", p=128)),
                             (wk0_sb, wk0.rearrange("(c p) n -> p c n", p=128)),
                             (wv0_sb, wv0.rearrange("(c p) n -> p c n", p=128)),
                             (wqkv_sb, w_qkv.rearrange("(c p) n -> p c n", p=128)),
                             (wproj_sb, w_proj.rearrange("(c p) n -> p c n", p=128)),
                             (bias_bc, b_proj.rearrange("(a n) -> a n", a=1).to_broadcast([128, D])),
                             (gamma_bc, gamma.rearrange("(a n) -> a n", a=1).to_broadcast([128, D])),
                             (beta_bc, beta.rearrange("(a n) -> a n", a=1).to_broadcast([128, D]))):
                sp.dma_start(dst[:], src).then_inc(weights_loaded, 16)
            for b in range(2):
                sp.dma_start(x_sb[b][:], x_pairs[b]).then_inc(x_loaded[b], 16)

            def step(t, b):
                count = counts(sp, t)
                if present(t, 2):
                    wait(sp, y0_done, count(1))
                    sp.dma_start(x_sb[b][:], x_pairs[t + 2]).then_inc(x_loaded[b], 16)
                if present(t, -2):
                    wait(sp, x2_done, count(-1))
                    sp.dma_start(out_pairs[t - 2], x2[b][:]).then_inc(x2_stored[b], 16)
            run_steps(sp, step)
            for b in range(2):
                sp.wait_ge(x2_stored[b], 16 * PAIRS // 2)

        @block.gpsimd
        def _(pool):
            nc.gpsimd.memset(ident[:], 0.0).then_inc(ident_zeroed, 1)
            nc.gpsimd.memset(eps_c[:], EPS).then_inc(pool_consts, 1)
            nc.gpsimd.memset(mhalf_c[:], -0.5).then_inc(pool_consts, 1)
            pool.wait_ge(ident_zeroed, 1)
            nc.gpsimd.affine_select(out=ident[:], in_=ident[:], compare_op=ALU.not_equal, fill=1.0, base=0,
                                    pattern=[[-1, 128]], channel_multiplier=1).then_inc(ident_ready, 1)
            pool.wait_ge(pool_consts, 2)
            pool.wait_ge(setup_done, 1)

            def inv_sqrt(mv, ve, ve_done, rstd, rstd_done, mv_ready, rstd_free, value):
                wait(pool, mv_ready, value)
                nc.gpsimd.tensor_tensor(ve[:], mv[:, :, 1], eps_c[:], ALU.add).then_inc(ve_done, 1)
                wait(pool, ve_done, value)
                nc.gpsimd.tensor_tensor(rstd[:], ve[:], mhalf_c[:], ALU.pow).then_inc(rstd_done, 1)

            def step(t, b):
                count = counts(pool, t)
                if present(t, -1):
                    wait(pool, x1_done, count(0))
                    wait(pool, ores_done, count(-2))
                    nc.gpsimd.tensor_tensor(x1b[1 - b][:], x1[1 - b][:], beta2[:], ALU.add).then_inc(x1b_done, 1)
                if present(t, 0):
                    wait(pool, ssq_done, count(1))
                    nc.gpsimd.tensor_tensor(rnorm[:], ssq[:], mhalf_c[:], ALU.pow).then_inc(rnorm_done, 1)
                    inv_sqrt(mv0, ve0, ve0_done, rstd0, rstd0_done, mv0_done, x1_done, count(1))

                def normalise(r):
                    wait(pool, rinv_done[r], count(0))
                    nc.gpsimd.tensor_tensor(prob[1 - b][:, r], prob[1 - b][:, r],
                                            rinv[:, r].unsqueeze(2).to_broadcast([N, J, N]),
                                            ALU.mult).then_inc(prob_done[r], 1)
                if present(t, -1):
                    normalise(0)
                    normalise(1)
                if present(t, -2):
                    wait(pool, o_done, count(-1))
                    nc.gpsimd.tensor_tensor(ores[:], o_sb[:], x1b[b][:], ALU.add).then_inc(ores_done, 1)
                    inv_sqrt(mv1, ve1, ve1_done, rstd1, rstd1_done, mv1_done, y1_done, count(-1))
                if present(t, -1):
                    normalise(2)
                if present(t, -2):
                    inv_sqrt(mv2, ve2, ve2_done, rstd2, rstd2_done, mv2_done, x2_done, count(-1))
                if present(t, -1):
                    normalise(3)
            run_steps(pool, step)

        @block.scalar
        def _(act):
            act.wait_ge(setup_done, 1)

            def copy_xT(value):
                wait(act, xT_made, value(1))
                nc.scalar.copy(xT_hi[:].rearrange("p c s n -> p (c s n)"), xT_bank[:]).then_inc(xT_hi_done, 1)

            copy_xT(lambda c: 1)

            def step(t, b):
                count = counts(act, t)

                def copy_pT(r, bank):
                    wait(act, pT_made[r], count(-1))
                    wait(act, oT_made, count(-2))
                    nc.scalar.copy(pT[:, r].rearrange("p j n -> p (j n)"), bank[:]).then_inc(pT_done[r], 1)

                def exps(r):
                    wait(act, max_done[r], count(0))
                    wait(act, pT_made[r], count(-2))
                    for j in range(J):
                        last = nc.scalar.activation(prob[1 - b][:, r, j], score[r][:, j], ACT.Exp,
                                                    bias=nmax[:, r, j:j + 1], accum_out=rsum[:, r, j:j + 1])
                    last.then_inc(exp_done[r], 1)

                if present(t, 0):
                    wait(act, u_made, count(1))
                    wait(act, vr_made[1], count(0))
                    nc.scalar.copy(wu_hi[:, :, :, D:D + N],
                                   u_bank[:].rearrange("p (c s n) -> p c s n", c=C, s=S)).then_inc(u_hi_done, 1)
                if present(t, -2):
                    copy_pT(0, pt01_bank[0])
                    copy_pT(1, pt01_bank[1])
                if present(t, 0):
                    for s in range(S):
                        wait(act, vr_made[s], count(1))
                        wait(act, o0_made, count(0))
                        nc.scalar.copy(v0_sb[:, s], vr_bank[s][:, 0:D]).then_inc(v0_done[s], 1)
                    wait(act, rel_made, count(1))
                    for s in range(S):
                        last = nc.scalar.activation(sq_junk[:, s], rt_bank[:, s * N:(s + 1) * N], ACT.Square,
                                                    accum_out=ssq[:, s:s + 1])
                    last.then_inc(ssq_done, 1)
                if present(t, -1):
                    exps(0)
                if present(t, -2):
                    copy_pT(2, pt23_bank[0])
                    copy_pT(3, pt23_bank[1])
                    wait(act, oT_made, count(-1))
                    wait(act, pr_made, count(-2))
                    nc.scalar.copy(oT_hi[:].rearrange("p s c n -> p (s c n)"), ot_bank[:]).then_inc(oT_hi_done, 1)
                if present(t, -1):
                    exps(1)
                if present(t, 0):
                    wait(act, x1T_made, count(1))
                    nc.scalar.copy(x1T_hi[:].rearrange("p c s n -> p (c s n)"), x1T_bank[:]).then_inc(x1T_hi_done, 1)
                if present(t, -1):
                    exps(2)
                    exps(3)
                if present(t, 0):
                    wait(act, q_made, count(1))
                    nc.scalar.copy(qT[:].rearrange("p c s n -> p (c s n)"), q_bank[:]).then_inc(q_done, 1)
                    wait(act, k_made, count(1))
                    nc.scalar.copy(kT[:].rearrange("p c s n -> p (c s n)"), k_bank[:]).then_inc(k_done, 1)
                    wait(act, v1_made, count(1))
                    wait(act, oT_made, count(-1))
                    nc.scalar.copy(v1[b][:].rearrange("p s n -> p (s n)"), v1_bank[:]).then_inc(v1_done, 1)
                if present(t, 1):
                    copy_xT(lambda c: count(1 + c))
            run_steps(act, step)

        @block.vector
        def _(dve):
            steps = [0]

            def in_turn(instruction):
                steps[0] += 1
                instruction.then_inc(setup_step, 1)
                dve.wait_ge(setup_step, steps[0])

            def split(hi, lo, full):
                in_turn(nc.vector.tensor_copy(hi, full))
                in_turn(nc.vector.tensor_tensor(lo, full, hi.bitcast(fp32), ALU.subtract))

            dve.wait_ge(weights_loaded, 9 * 16)
            dve.wait_ge(ident_ready, 1)
            nc.vector.tensor_copy(ident_bf[:], ident[:])
            nc.vector.tensor_scalar(mask_bf[:], adj_sb[:].unsqueeze(1).to_broadcast([N, J, N]),
                                    0.0, MASKED, ALU.is_equal, ALU.mult)
            nc.vector.tensor_copy(bias2[:], bias_bc[:].unsqueeze(1).to_broadcast([128, S, D]))
            nc.vector.tensor_copy(beta2[:], beta_bc[:].unsqueeze(1).to_broadcast([128, S, D]))
            in_turn(nc.vector.tensor_scalar(wqkv_sb[:, :, 0:D], wqkv_sb[:, :, 0:D], SCALE, None, ALU.mult))
            split(wqk_hi[:], wqk_lo[:], wqkv_sb[:, :, 0:2 * D])
            split(wv1_hi[:], wv1_lo[:], wqkv_sb[:, :, 2 * D:3 * D])
            split(wp_hi[:], wp_lo[:], wproj_sb[:])
            dve.wait_ge(m_made, 1)
            split(m_hi[:], m_lo[:], work[0][:].rearrange("p (c n) -> p c n", c=C))
            dve.wait_ge(wvT_made, 1)
            for s in range(S):
                split(wu_hi[:, :, s, 0:D], wu_lo[:, :, s, 0:D], work[1][:].rearrange("p (c n) -> p c n", c=C))
            nc.vector.memset(st0[:], 0.0).then_inc(setup_done, 1)

            def split_xT(value):
                wait(dve, xT_hi_done, value)
                nc.vector.tensor_tensor(xT_lo[:].rearrange("p c s n -> p (c s n)"), xT_bank[:],
                                        xT_hi[:].bitcast(fp32).rearrange("p c s n -> p (c s n)"),
                                        ALU.subtract).then_inc(xT_lo_done, 1)

            split_xT(1)

            def step(t, b):
                count = counts(dve, t)

                def norm_stats(y, st, mv, st_done, mv_done, value):
                    for s in range(S):
                        last = nc.vector.bn_stats(st[:, s], y[:, s])
                    last.then_inc(st_done, 1)
                    dve.wait_ge(setup_done, 1)
                    wait(dve, st_done, value)
                    for s in range(S):
                        last = nc.vector.bn_aggr(mv[:, s], st[:, s])
                    last.then_inc(mv_done, 1)

                def maxes(r):
                    wait(dve, exp_done[r], count(-1))
                    nc.vector.tensor_reduce(nmax[:, r], score[r][:], AX.X, ALU.max,
                                            negate=True).then_inc(max_done[r], 1)

                def inverses(r):
                    wait(dve, exp_done[r], count(0))
                    wait(dve, prob_done[r], count(-1))
                    nc.vector.reciprocal(rinv[:, r], rsum[:, r]).then_inc(rinv_done[r], 1)

                if present(t, 0):
                    wait(dve, u_hi_done, count(1))
                    nc.vector.tensor_tensor(wu_lo[:, :, :, D:D + N],
                                            u_bank[:].rearrange("p (c s n) -> p c s n", c=C, s=S),
                                            wu_hi[:, :, :, D:D + N].bitcast(fp32), ALU.subtract).then_inc(u_lo_done, 1)
                    for s in range(S):
                        wait(dve, v0_done[s], count(1))
                        nc.vector.tensor_tensor(relm[:, s], vr_bank[s][:, D:D + N], adj_sb[:],
                                                ALU.mult).then_inc(relm_done[s], 1)
                if present(t, -1):
                    wait(dve, scores_made, count(0))
                    maxes(0)
                    maxes(1)
                if present(t, 0):
                    wait(dve, o0_made, count(1))
                    wait(dve, rnorm_done, count(1))
                    for s in range(S):
                        last = nc.vector.scalar_tensor_tensor(y0[:, s], o0_bank[:, s * D:(s + 1) * D], rnorm[:, s:s + 1],
                                                              x_sb[b][:, s], ALU.mult, ALU.add)
                    last.then_inc(y0_done, 1)
                    wait(dve, y0_done, count(1))
                    norm_stats(y0, st0, mv0, st0_done, mv0_done, count(1))
                if present(t, -1):
                    maxes(2)
                    maxes(3)
                if present(t, 0):
                    wait(dve, rstd0_done, count(1))
                    wait(dve, x1b_done, count(-1))
                    for s in range(S):
                        last = nc.vector.tensor_scalar(x1[b][:, s], y0[:, s], mv0[:, s, 0:1], rstd0[:, s:s + 1],
                                                       ALU.subtract, ALU.mult)
                    last.then_inc(x1_done, 1)
                if present(t, -2):
                    wait(dve, oT_hi_done, count(-1))
                    nc.vector.tensor_tensor(oT_lo[:].rearrange("p s c n -> p (s c n)"), ot_bank[:],
                                            oT_hi[:].bitcast(fp32).rearrange("p s c n -> p (s c n)"),
                                            ALU.subtract).then_inc(oT_lo_done, 1)
                if present(t, 0):
                    wait(dve, x1T_hi_done, count(1))
                    nc.vector.tensor_tensor(x1T_lo[:].rearrange("p c s n -> p (c s n)"), x1T_bank[:],
                                            x1T_hi[:].bitcast(fp32).rearrange("p c s n -> p (c s n)"),
                                            ALU.subtract).then_inc(x1T_lo_done, 1)
                if present(t, -1):
                    inverses(0)
                if present(t, -2):
                    wait(dve, pr_made, count(-1))
                    wait(dve, ores_done, count(-2))
                    nc.vector.tensor_tensor(o_sb[:].rearrange("p s n -> p (s n)"), pr_bank[:],
                                            bias2[:].rearrange("p s n -> p (s n)"), ALU.add).then_inc(o_done, 1)
                    wait(dve, o_done, count(-1))
                    norm_stats(o_sb, st1, mv1, st1_done, mv1_done, count(-1))
                    wait(dve, mv1_done, count(-1))
                    for s in range(S):
                        last = nc.vector.scalar_tensor_tensor(og[:, s], o_sb[:, s], mv1[:, s, 0:1], gamma_bc[:],
                                                              ALU.subtract, ALU.mult)
                    last.then_inc(og_done, 1)
                if present(t, -1):
                    inverses(1)
                if present(t, -2):
                    wait(dve, og_done, count(-1))
                    wait(dve, rstd1_done, count(-1))
                    wait(dve, ores_done, count(-1))
                    for s in range(S):
                        last = nc.vector.scalar_tensor_tensor(y1[:, s], og[:, s], rstd1[:, s:s + 1], ores[:, s],
                                                              ALU.mult, ALU.add)
                    last.then_inc(y1_done, 1)
                    wait(dve, y1_done, count(-1))
                    norm_stats(y1, st2, mv2, st2_done, mv2_done, count(-1))
                if present(t, -1):
                    inverses(2)
                if present(t, -2):
                    wait(dve, rstd2_done, count(-1))
                    wait(dve, x2_stored[b], dma_count(dve, t, -4, b))
                    for s in range(S):
                        last = nc.vector.tensor_scalar(x2[b][:, s], y1[:, s], mv2[:, s, 0:1], rstd2[:, s:s + 1],
                                                       ALU.subtract, ALU.mult)
                    last.then_inc(x2_done, 1)
                if present(t, 1):
                    split_xT(count(2))
                if present(t, -1):
                    inverses(3)
            run_steps(dve, step)

        @block.tensor
        def _(pe):
            pe.wait_ge(weights_loaded, 9 * 16)
            pe.wait_ge(ident_ready, 1)
            for a in range(C):
                for e in range(C):
                    last = nc.tensor.matmul(work[0][:, a * D:(a + 1) * D], wq0_sb[:, e, a * 128:(a + 1) * 128],
                                            wk0_sb[:, e, :], start=(e == 0), stop=(e == C - 1))
            last.then_inc(m_made, 1)
            for c in range(C):
                for e in range(C):
                    last = nc.tensor.transpose(work[1][:, c * D + e * 128:c * D + (e + 1) * 128],
                                               wv0_sb[:, e, c * 128:(c + 1) * 128], ident[:])
            last.then_inc(wvT_made, 1)
            pe.wait_ge(setup_done, 1)

            def matmul_split(bank, lhs, rhs):
                passes = [(lhs[0], rhs[0]), (lhs[1], rhs[0]), (lhs[0], rhs[1])]
                for n, (l, r) in enumerate(passes):
                    for c in range(C):
                        last = nc.tensor.matmul(bank, l(c), r(c), start=(n == 0 and c == 0),
                                                stop=(n == 2 and c == C - 1))
                return last

            def transpose_x(src, bank, made):
                for c in range(C):
                    for s in range(S):
                        last = nc.tensor.transpose(bank[:, (c * S + s) * N:(c * S + s + 1) * N],
                                                   src[:, s, c * 128:(c + 1) * 128], ident[:])
                last.then_inc(made, 1)

            pe.wait_ge(x_loaded[0], 16)
            transpose_x(x_sb[0], xT_bank, xT_made)

            def step(t, b):
                count = counts(pe, t)

                def mask_scores():
                    for r in range(R):
                        wait(pe, exp_done[r], count(-1))
                        nc.tensor.matmul(score[r][:], ident_bf[:], mask_bf[:], start=True, stop=False,
                                         skip_group_check=True)

                def scores(s, c):
                    j = s * C + c
                    for r in range(R):
                        last = nc.tensor.matmul(score[r][:, j], qT[HD * r:HD * (r + 1), c, s, :],
                                                kT[HD * r:HD * (r + 1), c, s, :], start=False, stop=True,
                                                skip_group_check=True)
                    return last

                def transpose_probs(r, bank, bank_free, value):
                    wait(pe, prob_done[r], count(-1))
                    wait(pe, bank_free, value)
                    for j in range(J):
                        last = nc.tensor.transpose(bank[:, j * N:(j + 1) * N], prob[b][:, r, j], ident[:])
                    last.then_inc(pT_made[r], 1)

                A, B, CC = present(t, 0), present(t, -1), present(t, -2)
                if B:
                    wait(pe, q_done, count(0))
                    wait(pe, k_done, count(0))
                    mask_scores()
                    scores(0, 0)
                if A:
                    wait(pe, xT_lo_done, count(1))
                    wait(pe, q_done, count(0))
                    for u in range(C):
                        last = matmul_split(u_bank[:, u * S * N:(u + 1) * S * N],
                                            [lambda c: m_hi[:, c, u * 128:(u + 1) * 128],
                                             lambda c: m_lo[:, c, u * 128:(u + 1) * 128]],
                                            [lambda c: xT_hi[:, c].rearrange("p s n -> p (s n)"),
                                             lambda c: xT_lo[:, c].rearrange("p s n -> p (s n)")])
                    last.then_inc(u_made, 1)
                if B:
                    scores(0, 1)
                if CC:
                    transpose_probs(0, pt01_bank[0], k_done, count(0))
                    transpose_probs(1, pt01_bank[1], v1_done, count(0))
                if B:
                    scores(1, 0)
                if A:
                    wait(pe, u_lo_done, count(1))
                    for s in range(S):
                        last = matmul_split(vr_bank[s][:, 0:D + N],
                                            [lambda c: xT_hi[:, c, s], lambda c: xT_lo[:, c, s]],
                                            [lambda c: wu_hi[:, c, s], lambda c: wu_lo[:, c, s]])
                        last.then_inc(vr_made[s], 1)
                if B:
                    scores(1, 1).then_inc(scores_made, 1)
                if A:
                    wait(pe, pT_done[0], count(-1))
                    for s in range(S):
                        wait(pe, relm_done[s], count(1))
                        last = nc.tensor.transpose(rt_bank[:, s * N:(s + 1) * N], relm[:, s], ident[:])
                    last.then_inc(rel_made, 1)
                    wait(pe, pT_done[1], count(-1))
                    for s in range(S):
                        wait(pe, v0_done[s], count(1))
                        last = nc.tensor.matmul(o0_bank[:, s * D:(s + 1) * D], relm[:, s], v0_sb[:, s],
                                                start=True, stop=True)
                    last.then_inc(o0_made, 1)
                if CC:
                    transpose_probs(2, pt23_bank[0], relm_done[0], count(1))
                    transpose_probs(3, pt23_bank[1], relm_done[1], count(1))
                    wait(pe, ssq_done, count(1))
                    wait(pe, v1_done, count(-1))
                    for r in range(R):
                        wait(pe, pT_done[r], count(-1))
                    for s in range(S):
                        for c in range(C):
                            j = s * C + c
                            for r in range(R):
                                h = c * R + r
                                last = nc.tensor.matmul(ot_bank[HD * r:HD * (r + 1), j * N:(j + 1) * N],
                                                        v1[b][:, s, h * HD:(h + 1) * HD], pT[:, r, j],
                                                        start=True, stop=True)
                    last.then_inc(oT_made, 1)
                if A:
                    wait(pe, x1_done, count(1))
                    transpose_x(x1[b], x1T_bank, x1T_made)
                if CC:
                    wait(pe, oT_lo_done, count(-1))
                    wait(pe, pT_done[2], count(-1))
                    for s in range(S):
                        last = matmul_split(pr_bank[:, s * D:(s + 1) * D],
                                            [lambda c: oT_hi[:, s, c], lambda c: oT_lo[:, s, c]],
                                            [lambda c: wp_hi[:, c], lambda c: wp_lo[:, c]])
                    last.then_inc(pr_made, 1)
                if A:
                    wait(pe, x1T_lo_done, count(1))
                    wait(pe, pT_done[3], count(-1))
                    for part, bank, made, last_use in ((0, q_bank, q_made, None), (1, k_bank, k_made, oT_lo_done)):
                        if last_use is not None:
                            wait(pe, last_use, count(-1))
                        for u in range(C):
                            at = part * D + u * 128
                            last = matmul_split(bank[:, u * S * N:(u + 1) * S * N],
                                                [lambda c: wqk_hi[:, c, at:at + 128],
                                                 lambda c: wqk_lo[:, c, at:at + 128]],
                                                [lambda c: x1T_hi[:, c].rearrange("p s n -> p (s n)"),
                                                 lambda c: x1T_lo[:, c].rearrange("p s n -> p (s n)")])
                        last.then_inc(made, 1)
                    for s in range(S):
                        last = matmul_split(v1_bank[:, s * D:(s + 1) * D],
                                            [lambda c: x1T_hi[:, c, s], lambda c: x1T_lo[:, c, s]],
                                            [lambda c: wv1_hi[:, c], lambda c: wv1_lo[:, c]])
                    last.then_inc(v1_made, 1)
                if present(t, 1):
                    wait(pe, x_loaded[1 - b], dma_count(pe, t, 1, 1 - b))
                    wait(pe, o_done, count(-1))
                    transpose_x(x_sb[1 - b], xT_bank, xT_made)
            run_steps(pe, step)


_INS = ['x', 'adj', 'L0_gnn_Wq', 'L0_gnn_Wk', 'L0_gnn_Wv', 'L1_gnn_w_qkv', 'L1_gnn_w_proj',
        'L1_gnn_b_proj', 'L1_gnn_ln_gamma', 'L1_gnn_ln_beta']
_OUTS = [((64, 128, 256), 'float32')]


def kernel(**inputs):
    import numpy as _np
    import concourse.bacc as _bacc
    from concourse import mybir as _mybir
    from concourse.bass_utils import run_bass_kernel_spmd as _run

    nc = _bacc.Bacc("TRN2", target_bir_lowering=False, num_devices=1)
    arrays, args = {}, []
    for name in _INS:
        a = _np.ascontiguousarray(inputs[name])
        arrays[f"in_{name}_dram"] = a
        args.append(nc.dram_tensor(f"in_{name}_dram", a.shape, _mybir.dt.from_np(a.dtype), kind="ExternalInput").ap())
    for i, (shape, dtype) in enumerate(_OUTS):
        dt = _mybir.dt.from_np(_np.dtype(dtype))
        args.append(nc.dram_tensor(f"out_{i}_dram", shape, dt, kind="ExternalOutput").ap())
    gnn_two_layer_kernel(nc, *args)
    r = _run(nc, [arrays], core_ids=[0])
    got = tuple(r.results[0][f"out_{i}_dram"] for i in range(len(_OUTS)))
    return got[0]
```

```python
import concourse.bass as bass
from concourse import mybir
from contextlib import ExitStack


def gnn_two_layer_kernel(nc, x, adj, wq0, wk0, wv0, w_qkv, w_proj, b_proj, gamma, beta, out):
    fp32 = mybir.dt.float32
    f32r = mybir.dt.float32r
    bf16 = mybir.dt.bfloat16
    ALU = mybir.AluOpType
    ACT = mybir.ActivationFunctionType
    AX = mybir.AxisListType

    BATCH, N, D = x.shape
    H = 8
    HD = D // H
    S = 2
    C = D // 128
    R = 128 // HD
    J = S * C
    PAIRS = BATCH // S
    HALF = C * S * N // 2
    EPS = 1e-5
    SCALE = float(HD) ** -0.5
    MASKED = -1e30
    LOOP_FROM, LOOP_TO = 4, PAIRS - 2

    x_pairs = x.rearrange("(p s) n d -> p n s d", s=S)
    out_pairs = out.rearrange("(p s) n d -> p n s d", s=S)

    ctx = ExitStack()
    with ctx:
        def sb(name, shape, dt=fp32):
            return ctx.enter_context(nc.sbuf_tensor(name, shape, dt))

        def sem(name):
            return ctx.enter_context(nc.semaphore(name))

        wq0_sb = sb("wq0_sb", [128, C, D])
        wk0_sb = sb("wk0_sb", [128, C, D])
        wv0_sb = sb("wv0_sb", [128, C, D])
        wqkv_sb = sb("wqkv_sb", [128, C, 3 * D])
        wproj_sb = sb("wproj_sb", [128, C, D])
        adj_sb = sb("adj_sb", [N, N])
        bias_bc = sb("bias_bc", [128, D])
        bias2 = sb("bias2", [128, S, D])
        gamma_bc = sb("gamma_bc", [128, D])
        beta_bc = sb("beta_bc", [128, D])
        beta2 = sb("beta2", [128, S, D])
        ident = sb("ident", [128, 128])
        ident_bf = sb("ident_bf", [128, 128], bf16)
        mask_bf = sb("mask_bf", [N, J, N], bf16)
        eps_c = sb("eps_c", [128, S])
        mhalf_c = sb("mhalf_c", [128, S])
        m_hi = sb("m_hi", [128, C, D], f32r)
        m_lo = sb("m_lo", [128, C, D], f32r)
        wu_hi = sb("wu_hi", [128, C, S, D + N], f32r)
        wu_lo = sb("wu_lo", [128, C, S, D + N], f32r)
        wqk_hi = sb("wqk_hi", [128, C, 2 * D], f32r)
        wqk_lo = sb("wqk_lo", [128, C, 2 * D], f32r)
        wv1_hi = sb("wv1_hi", [128, C, D], f32r)
        wv1_lo = sb("wv1_lo", [128, C, D], f32r)
        wp_hi = sb("wp_hi", [128, C, D], f32r)
        wp_lo = sb("wp_lo", [128, C, D], f32r)

        x_sb = [sb(f"x_sb{b}", [N, S, D]) for b in range(2)]
        xT_hi = sb("xT_hi", [128, C, S, N], f32r)
        xT_lo = sb("xT_lo", [128, C, S, N], f32r)
        v0_sb = sb("v0_sb", [N, S, D])
        relm = sb("relm", [N, S, N])
        sq_junk = sb("sq_junk", [N, S, N])
        ssq = sb("ssq", [N, S])
        rnorm = sb("rnorm", [N, S])
        y0 = sb("y0", [N, S, D])
        st0 = sb("st0", [N, S, 6])
        mv0 = sb("mv0", [N, S, 2])
        ve0 = sb("ve0", [N, S])
        rstd0 = sb("rstd0", [N, S])
        x1 = [sb(f"x1_{b}", [N, S, D]) for b in range(2)]
        x1b = [sb(f"x1b_{b}", [N, S, D]) for b in range(2)]
        x1T_hi = sb("x1T_hi", [128, C, S, N], f32r)
        x1T_lo = sb("x1T_lo", [128, C, S, N], f32r)
        qT = sb("qT", [128, C, S, N])
        kT = sb("kT", [128, C, S, N])
        v1 = [sb(f"v1_{b}", [N, S, D]) for b in range(2)]
        nmax = sb("nmax", [N, R, J])
        rsum = sb("rsum", [N, R, J])
        rinv = sb("rinv", [N, R, J])
        prob = [sb(f"prob{b}", [N, R, J, N]) for b in range(2)]
        pT = sb("pT", [N, R, J, N])
        oT_hi = sb("oT_hi", [128, S, C, N], f32r)
        oT_lo = sb("oT_lo", [128, S, C, N], f32r)
        o_sb = sb("o_sb", [N, S, D])
        ores = sb("ores", [N, S, D])
        og = sb("og", [N, S, D])
        y1 = sb("y1", [N, S, D])
        st1 = sb("st1", [N, S, 6])
        mv1 = sb("mv1", [N, S, 2])
        ve1 = sb("ve1", [N, S])
        rstd1 = sb("rstd1", [N, S])
        st2 = sb("st2", [N, S, 6])
        mv2 = sb("mv2", [N, S, 2])
        ve2 = sb("ve2", [N, S])
        rstd2 = sb("rstd2", [N, S])
        x2 = [sb(f"x2_{b}", [N, S, D]) for b in range(2)]

        score = [ctx.enter_context(nc.psum_tensor(f"score{r}", [128, J, N], fp32)) for r in range(R)]
        work = [ctx.enter_context(nc.psum_tensor(f"work{b}", [128, 512], fp32)) for b in range(4)]
        v1_bank, vr_bank, rt_bank = work[0], [work[1], work[2]], work[3]
        o0_bank = work[0]
        pT_bank = [work[1], work[2], work[3], work[0]]
        xT_bank, ot_bank, u_bank = work[1], work[2], work[3]
        x1T_bank, pr_bank, q_bank, k_bank = work[0], work[1], work[2], work[3]

        weights_loaded = sem("weights_loaded")
        ident_zeroed = sem("ident_zeroed")
        ident_ready = sem("ident_ready")
        pool_consts = sem("pool_consts")
        m_made = sem("m_made")
        wvT_made = sem("wvT_made")
        setup_step = sem("setup_step")
        setup_done = sem("setup_done")
        x_loaded = [sem(f"x_loaded{b}") for b in range(2)]
        x2_stored = [sem(f"x2_stored{b}") for b in range(2)]
        xT_made = sem("xT_made")
        u_made = sem("u_made")
        vr_made = [sem(f"vr_made{s}") for s in range(S)]
        rel_made = sem("rel_made")
        o0_made = sem("o0_made")
        x1T_made = sem("x1T_made")
        q_made = sem("q_made")
        k_made = sem("k_made")
        v1_made = sem("v1_made")
        scores_made = sem("scores_made")
        pT_made = [sem(f"pT_made{r}") for r in range(R)]
        oT_made = sem("oT_made")
        pr_made = sem("pr_made")
        xT_hi_done = sem("xT_hi_done")
        u_hi_done = sem("u_hi_done")
        v0_done = [sem(f"v0_done{s}") for s in range(S)]
        ssq_done = sem("ssq_done")
        x1T_hi_done = sem("x1T_hi_done")
        q_done = sem("q_done")
        k_done = sem("k_done")
        v1_done = sem("v1_done")
        exp_done = [sem(f"exp_done{r}") for r in range(R)]
        pT_done = [sem(f"pT_done{r}") for r in range(R)]
        oT_hi_done = sem("oT_hi_done")
        xT_lo_done = sem("xT_lo_done")
        u_lo_done = sem("u_lo_done")
        relm_done = [sem(f"relm_done{s}") for s in range(S)]
        y0_done = sem("y0_done")
        st0_done = sem("st0_done")
        mv0_done = sem("mv0_done")
        x1_done = sem("x1_done")
        x1T_lo_done = sem("x1T_lo_done")
        max_done = [sem(f"max_done{r}") for r in range(R)]
        rinv_done = [sem(f"rinv_done{r}") for r in range(R)]
        oT_lo_done = sem("oT_lo_done")
        o_done = sem("o_done")
        st1_done = sem("st1_done")
        mv1_done = sem("mv1_done")
        og_done = sem("og_done")
        y1_done = sem("y1_done")
        st2_done = sem("st2_done")
        mv2_done = sem("mv2_done")
        x2_done = sem("x2_done")
        rnorm_done = sem("rnorm_done")
        ve0_done = sem("ve0_done")
        rstd0_done = sem("rstd0_done")
        x1b_done = sem("x1b_done")
        prob_done = [sem(f"prob_done{r}") for r in range(R)]
        ores_done = sem("ores_done")
        ve1_done = sem("ve1_done")
        rstd1_done = sem("rstd1_done")
        ve2_done = sem("ve2_done")
        rstd2_done = sem("rstd2_done")

        def wait(eng, semaphore, count):
            if not (isinstance(count, int) and count <= 0):
                eng.wait_ge(semaphore, count)

        def counts(eng, t):
            kept = {}

            def count(c):
                if isinstance(t, int):
                    return min(t + c, PAIRS)
                if c not in kept:
                    kept[c] = eng.snap(t + c)
                return kept[c]
            return count

        def dma_count(eng, t, c, b):
            if isinstance(t, int):
                return 8 * (t + c - b) + 16
            return eng.snap(8 * t + (8 * (c - b) + 16))

        def run_steps(eng, step):
            for t in range(LOOP_FROM):
                step(t, t % 2)
            with eng.Fori(LOOP_FROM, LOOP_TO - 1, 2) as t:
                step(t, 0)
                step(t + 1, 1)
            for t in range(LOOP_TO, PAIRS + 2):
                step(t, t % 2)

        def present(t, c):
            return not isinstance(t, int) or 0 <= t + c < PAIRS

        block = ctx.enter_context(nc.Block())

        @block.sync
        def _(sp):
            for dst, src in ((adj_sb, adj),
                             (wq0_sb, wq0.rearrange("(c p) n -> p c n", p=128)),
                             (wk0_sb, wk0.rearrange("(c p) n -> p c n", p=128)),
                             (wv0_sb, wv0.rearrange("(c p) n -> p c n", p=128)),
                             (wqkv_sb, w_qkv.rearrange("(c p) n -> p c n", p=128)),
                             (wproj_sb, w_proj.rearrange("(c p) n -> p c n", p=128)),
                             (bias_bc, b_proj.rearrange("(a n) -> a n", a=1).to_broadcast([128, D])),
                             (gamma_bc, gamma.rearrange("(a n) -> a n", a=1).to_broadcast([128, D])),
                             (beta_bc, beta.rearrange("(a n) -> a n", a=1).to_broadcast([128, D]))):
                sp.dma_start(dst[:], src).then_inc(weights_loaded, 16)
            for b in range(2):
                sp.dma_start(x_sb[b][:], x_pairs[b]).then_inc(x_loaded[b], 16)

            def step(t, b):
                count = counts(sp, t)
                if present(t, 2):
                    wait(sp, y0_done, count(1))
                    sp.dma_start(x_sb[b][:], x_pairs[t + 2]).then_inc(x_loaded[b], 16)
                if present(t, -2):
                    wait(sp, x2_done, count(-1))
                    sp.dma_start(out_pairs[t - 2], x2[b][:]).then_inc(x2_stored[b], 16)
            run_steps(sp, step)
            for b in range(2):
                sp.wait_ge(x2_stored[b], 16 * PAIRS // 2)

        @block.gpsimd
        def _(pool):
            nc.gpsimd.memset(ident[:], 0.0).then_inc(ident_zeroed, 1)
            nc.gpsimd.memset(eps_c[:], EPS).then_inc(pool_consts, 1)
            nc.gpsimd.memset(mhalf_c[:], -0.5).then_inc(pool_consts, 1)
            pool.wait_ge(ident_zeroed, 1)
            nc.gpsimd.affine_select(out=ident[:], in_=ident[:], compare_op=ALU.not_equal, fill=1.0, base=0,
                                    pattern=[[-1, 128]], channel_multiplier=1).then_inc(ident_ready, 1)
            pool.wait_ge(pool_consts, 2)
            pool.wait_ge(setup_done, 1)

            def inv_sqrt(mv, ve, ve_done, rstd, rstd_done, mv_ready, value):
                wait(pool, mv_ready, value)
                nc.gpsimd.tensor_tensor(ve[:], mv[:, :, 1], eps_c[:], ALU.add).then_inc(ve_done, 1)
                wait(pool, ve_done, value)
                nc.gpsimd.tensor_tensor(rstd[:], ve[:], mhalf_c[:], ALU.pow).then_inc(rstd_done, 1)

            def step(t, b):
                count = counts(pool, t)
                A, B, CC = present(t, 0), present(t, -1), present(t, -2)

                def normalise(r):
                    wait(pool, rinv_done[r], count(0))
                    nc.gpsimd.tensor_tensor(prob[1 - b][:, r], prob[1 - b][:, r],
                                            rinv[:, r].unsqueeze(2).to_broadcast([N, J, N]),
                                            ALU.mult).then_inc(prob_done[r], 1)
                if B:
                    wait(pool, x1_done, count(0))
                    wait(pool, ores_done, count(-2))
                    nc.gpsimd.tensor_tensor(x1b[1 - b][:], x1[1 - b][:], beta2[:], ALU.add).then_inc(x1b_done, 1)
                if A:
                    wait(pool, ssq_done, count(1))
                    nc.gpsimd.tensor_tensor(rnorm[:], ssq[:], mhalf_c[:], ALU.pow).then_inc(rnorm_done, 1)
                if B:
                    normalise(0)
                if A:
                    inv_sqrt(mv0, ve0, ve0_done, rstd0, rstd0_done, mv0_done, count(1))
                if B:
                    for r in range(1, R):
                        normalise(r)
                if CC:
                    wait(pool, o_done, count(-1))
                    nc.gpsimd.tensor_tensor(ores[:], o_sb[:], x1b[b][:], ALU.add).then_inc(ores_done, 1)
                    inv_sqrt(mv1, ve1, ve1_done, rstd1, rstd1_done, mv1_done, count(-1))
                    inv_sqrt(mv2, ve2, ve2_done, rstd2, rstd2_done, mv2_done, count(-1))
            run_steps(pool, step)

        @block.scalar
        def _(act):
            act.wait_ge(setup_done, 1)

            def copy_xT(count):
                wait(act, xT_made, count(2))
                nc.scalar.copy(xT_hi[:].rearrange("p c s n -> p (c s n)"), xT_bank[:]).then_inc(xT_hi_done, 1)

            def copy_u(count):
                wait(act, u_made, count(2))
                nc.scalar.copy(wu_hi[:, :, :, D:D + N],
                               u_bank[:].rearrange("p (c s n) -> p c s n", c=C, s=S)).then_inc(u_hi_done, 1)

            def step(t, b):
                count = counts(act, t)
                A, B, CC, NEXT = present(t, 0), present(t, -1), present(t, -2), present(t, 1)

                def copy_v0(s):
                    wait(act, relm_done[s], count(1))
                    wait(act, o0_made, count(0))
                    nc.scalar.copy(v0_sb[:, s], vr_bank[s][:, 0:D]).then_inc(v0_done[s], 1)

                def copy_pT(r):
                    wait(act, pT_made[r], count(-1))
                    wait(act, oT_made, count(-2))
                    nc.scalar.copy(pT[:, r].rearrange("p j n -> p (j n)"), pT_bank[r][:]).then_inc(pT_done[r], 1)

                def exps(r):
                    wait(act, max_done[r], count(0))
                    wait(act, pT_made[r], count(-2))
                    for j in range(J):
                        last = nc.scalar.activation(prob[1 - b][:, r, j], score[r][:, j], ACT.Exp,
                                                    bias=nmax[:, r, j:j + 1], accum_out=rsum[:, r, j:j + 1])
                    last.then_inc(exp_done[r], 1)

                if B:
                    wait(act, v1_made, count(0))
                    wait(act, oT_made, count(-2))
                    nc.scalar.copy(v1[1 - b][:].rearrange("p s n -> p (s n)"), v1_bank[:]).then_inc(v1_done, 1)
                    exps(0)
                if A:
                    copy_v0(0)
                    copy_v0(1)
                    wait(act, rel_made, count(1))
                    for s in range(S):
                        last = nc.scalar.activation(sq_junk[:, s], rt_bank[:, s * N:(s + 1) * N], ACT.Square,
                                                    accum_out=ssq[:, s:s + 1])
                    last.then_inc(ssq_done, 1)
                if B:
                    exps(1)
                if CC:
                    copy_pT(0)
                    copy_pT(1)
                    copy_pT(2)
                    copy_pT(3)
                if NEXT:
                    copy_xT(count)
                if B:
                    exps(2)
                if CC:
                    wait(act, oT_made, count(-1))
                    wait(act, pr_made, count(-2))
                    nc.scalar.copy(oT_hi[:].rearrange("p s c n -> p (s c n)"), ot_bank[:]).then_inc(oT_hi_done, 1)
                if NEXT:
                    copy_u(count)
                if A:
                    wait(act, x1T_made, count(1))
                    nc.scalar.copy(x1T_hi[:].rearrange("p c s n -> p (c s n)"), x1T_bank[:]).then_inc(x1T_hi_done, 1)
                if B:
                    exps(3)
                if A:
                    wait(act, q_made, count(1))
                    nc.scalar.copy(qT[:].rearrange("p c s n -> p (c s n)"), q_bank[:]).then_inc(q_done, 1)
                    wait(act, k_made, count(1))
                    nc.scalar.copy(kT[:].rearrange("p c s n -> p (c s n)"), k_bank[:]).then_inc(k_done, 1)
            copy_xT(lambda c: 1)
            copy_u(lambda c: 1)
            run_steps(act, step)

        @block.vector
        def _(dve):
            steps = [0]

            def in_turn(instruction):
                steps[0] += 1
                instruction.then_inc(setup_step, 1)
                dve.wait_ge(setup_step, steps[0])

            def split(hi, lo, full):
                in_turn(nc.vector.tensor_copy(hi, full))
                in_turn(nc.vector.tensor_tensor(lo, full, hi.bitcast(fp32), ALU.subtract))

            dve.wait_ge(weights_loaded, 9 * 16)
            dve.wait_ge(ident_ready, 1)
            nc.vector.tensor_copy(ident_bf[:], ident[:])
            nc.vector.tensor_scalar(mask_bf[:], adj_sb[:].unsqueeze(1).to_broadcast([N, J, N]),
                                    0.0, MASKED, ALU.is_equal, ALU.mult)
            nc.vector.tensor_copy(bias2[:], bias_bc[:].unsqueeze(1).to_broadcast([128, S, D]))
            nc.vector.tensor_copy(beta2[:], beta_bc[:].unsqueeze(1).to_broadcast([128, S, D]))
            in_turn(nc.vector.tensor_scalar(wqkv_sb[:, :, 0:D], wqkv_sb[:, :, 0:D], SCALE, None, ALU.mult))
            split(wqk_hi[:], wqk_lo[:], wqkv_sb[:, :, 0:2 * D])
            split(wv1_hi[:], wv1_lo[:], wqkv_sb[:, :, 2 * D:3 * D])
            split(wp_hi[:], wp_lo[:], wproj_sb[:])
            dve.wait_ge(m_made, 1)
            split(m_hi[:], m_lo[:], work[0][:].rearrange("p (c n) -> p c n", c=C))
            dve.wait_ge(wvT_made, 1)
            for s in range(S):
                split(wu_hi[:, :, s, 0:D], wu_lo[:, :, s, 0:D], work[1][:].rearrange("p (c n) -> p c n", c=C))
            nc.vector.memset(st0[:], 0.0).then_inc(setup_done, 1)

            def split_xT(value):
                wait(dve, xT_hi_done, value)
                nc.vector.tensor_tensor(xT_lo[:].rearrange("p c s n -> p (c s n)"), xT_bank[:],
                                        xT_hi[:].bitcast(fp32).rearrange("p c s n -> p (c s n)"),
                                        ALU.subtract).then_inc(xT_lo_done, 1)

            def split_u(value):
                wait(dve, u_hi_done, value)
                nc.vector.tensor_tensor(wu_lo[:, :, :, D:D + N],
                                        u_bank[:].rearrange("p (c s n) -> p c s n", c=C, s=S),
                                        wu_hi[:, :, :, D:D + N].bitcast(fp32), ALU.subtract).then_inc(u_lo_done, 1)

            split_xT(1)
            split_u(1)

            def step(t, b):
                count = counts(dve, t)

                def norm_stats(y, st, mv, st_done, mv_done, value):
                    for s in range(S):
                        last = nc.vector.bn_stats(st[:, s], y[:, s])
                    last.then_inc(st_done, 1)
                    dve.wait_ge(setup_done, 1)
                    wait(dve, st_done, value)
                    for s in range(S):
                        last = nc.vector.bn_aggr(mv[:, s], st[:, s])
                    last.then_inc(mv_done, 1)

                def maxes(r):
                    wait(dve, exp_done[r], count(-1))
                    nc.vector.tensor_reduce(nmax[:, r], score[r][:], AX.X, ALU.max,
                                            negate=True).then_inc(max_done[r], 1)

                def inverses(r):
                    wait(dve, exp_done[r], count(0))
                    wait(dve, prob_done[r], count(-1))
                    nc.vector.reciprocal(rinv[:, r], rsum[:, r]).then_inc(rinv_done[r], 1)

                def mask_rel(s):
                    wait(dve, vr_made[s], count(1))
                    nc.vector.tensor_tensor(relm[:, s], vr_bank[s][:, D:D + N], adj_sb[:],
                                            ALU.mult).then_inc(relm_done[s], 1)

                A, B, CC, NEXT = present(t, 0), present(t, -1), present(t, -2), present(t, 1)
                if B:
                    wait(dve, scores_made, count(0))
                    maxes(0)
                if A:
                    mask_rel(0)
                if B:
                    maxes(1)
                if A:
                    mask_rel(1)
                if B:
                    maxes(2)
                    maxes(3)
                    inverses(0)
                if A:
                    wait(dve, o0_made, count(1))
                    wait(dve, rnorm_done, count(1))
                    for s in range(S):
                        last = nc.vector.scalar_tensor_tensor(y0[:, s], o0_bank[:, s * D:(s + 1) * D], rnorm[:, s:s + 1],
                                                              x_sb[b][:, s], ALU.mult, ALU.add)
                    last.then_inc(y0_done, 1)
                    wait(dve, y0_done, count(1))
                    norm_stats(y0, st0, mv0, st0_done, mv0_done, count(1))
                if B:
                    inverses(1)
                if NEXT:
                    split_xT(count(2))
                if CC:
                    wait(dve, oT_hi_done, count(-1))
                    nc.vector.tensor_tensor(oT_lo[:].rearrange("p s c n -> p (s c n)"), ot_bank[:],
                                            oT_hi[:].bitcast(fp32).rearrange("p s c n -> p (s c n)"),
                                            ALU.subtract).then_inc(oT_lo_done, 1)
                if A:
                    wait(dve, rstd0_done, count(1))
                    wait(dve, x1b_done, count(-1))
                    for s in range(S):
                        last = nc.vector.tensor_scalar(x1[b][:, s], y0[:, s], mv0[:, s, 0:1], rstd0[:, s:s + 1],
                                                       ALU.subtract, ALU.mult)
                    last.then_inc(x1_done, 1)
                if B:
                    inverses(2)
                if NEXT:
                    split_u(count(2))
                if A:
                    wait(dve, x1T_hi_done, count(1))
                    nc.vector.tensor_tensor(x1T_lo[:].rearrange("p c s n -> p (c s n)"), x1T_bank[:],
                                            x1T_hi[:].bitcast(fp32).rearrange("p c s n -> p (c s n)"),
                                            ALU.subtract).then_inc(x1T_lo_done, 1)
                if B:
                    inverses(3)
                if CC:
                    wait(dve, pr_made, count(-1))
                    wait(dve, ores_done, count(-2))
                    nc.vector.tensor_tensor(o_sb[:].rearrange("p s n -> p (s n)"), pr_bank[:],
                                            bias2[:].rearrange("p s n -> p (s n)"), ALU.add).then_inc(o_done, 1)
                    wait(dve, o_done, count(-1))
                    norm_stats(o_sb, st1, mv1, st1_done, mv1_done, count(-1))
                    wait(dve, mv1_done, count(-1))
                    for s in range(S):
                        last = nc.vector.scalar_tensor_tensor(og[:, s], o_sb[:, s], mv1[:, s, 0:1], gamma_bc[:],
                                                              ALU.subtract, ALU.mult)
                    last.then_inc(og_done, 1)
                    wait(dve, og_done, count(-1))
                    wait(dve, rstd1_done, count(-1))
                    wait(dve, ores_done, count(-1))
                    for s in range(S):
                        last = nc.vector.scalar_tensor_tensor(y1[:, s], og[:, s], rstd1[:, s:s + 1], ores[:, s],
                                                              ALU.mult, ALU.add)
                    last.then_inc(y1_done, 1)
                    wait(dve, y1_done, count(-1))
                    norm_stats(y1, st2, mv2, st2_done, mv2_done, count(-1))
                    wait(dve, rstd2_done, count(-1))
                    wait(dve, x2_stored[b], dma_count(dve, t, -4, b))
                    for s in range(S):
                        last = nc.vector.tensor_scalar(x2[b][:, s], y1[:, s], mv2[:, s, 0:1], rstd2[:, s:s + 1],
                                                       ALU.subtract, ALU.mult)
                    last.then_inc(x2_done, 1)
            run_steps(dve, step)

        @block.tensor
        def _(pe):
            pe.wait_ge(weights_loaded, 9 * 16)
            pe.wait_ge(ident_ready, 1)
            for a in range(C):
                for e in range(C):
                    last = nc.tensor.matmul(work[0][:, a * D:(a + 1) * D], wq0_sb[:, e, a * 128:(a + 1) * 128],
                                            wk0_sb[:, e, :], start=(e == 0), stop=(e == C - 1))
            last.then_inc(m_made, 1)
            for c in range(C):
                for e in range(C):
                    last = nc.tensor.transpose(work[1][:, c * D + e * 128:c * D + (e + 1) * 128],
                                               wv0_sb[:, e, c * 128:(c + 1) * 128], ident[:])
            last.then_inc(wvT_made, 1)
            pe.wait_ge(setup_done, 1)

            def matmul_split(bank, passes, before_last=None):
                for n, (l, r) in enumerate(passes):
                    if n == 2 and before_last is not None:
                        before_last()
                    for c in range(C):
                        last = nc.tensor.matmul(bank, l(c), r(c), start=(n == 0 and c == 0),
                                                stop=(n == 2 and c == C - 1))
                return last

            def weights_times(bank, w_hi, w_lo, at, a_hi, a_lo, before_last=None):
                def weights(w):
                    return lambda c: w[:, c, at:at + 128]

                def tokens(a):
                    return lambda c: a[:, c].rearrange("p s n -> p (s n)")
                return matmul_split(bank, [(weights(w_hi), tokens(a_hi)), (weights(w_lo), tokens(a_hi)),
                                           (weights(w_hi), tokens(a_lo))], before_last)

            def transpose_x(src, bank, made):
                for c in range(C):
                    for s in range(S):
                        last = nc.tensor.transpose(bank[:, (c * S + s) * N:(c * S + s + 1) * N],
                                                   src[:, s, c * 128:(c + 1) * 128], ident[:])
                last.then_inc(made, 1)

            def project_u(count):
                wait(pe, xT_hi_done, count(2))
                for u in range(C):
                    last = weights_times(u_bank[:, u * S * N:(u + 1) * S * N], m_hi, m_lo, u * 128, xT_hi, xT_lo,
                                         lambda: wait(pe, xT_lo_done, count(2)) if u == 0 else None)
                last.then_inc(u_made, 1)

            pe.wait_ge(x_loaded[0], 16)
            transpose_x(x_sb[0], xT_bank, xT_made)
            project_u(lambda c: c - 1)

            def step(t, b):
                count = counts(pe, t)

                def mask_scores():
                    for r in range(R):
                        wait(pe, exp_done[r], count(-1))
                        nc.tensor.matmul(score[r][:], ident_bf[:], mask_bf[:], start=True, stop=False,
                                         skip_group_check=True)

                def scores(s, c):
                    j = s * C + c
                    for r in range(R):
                        last = nc.tensor.matmul(score[r][:, j], qT[HD * r:HD * (r + 1), c, s, :],
                                                kT[HD * r:HD * (r + 1), c, s, :], start=False, stop=True,
                                                skip_group_check=True)
                    return last

                def transpose_probs(r, bank_free, value):
                    wait(pe, prob_done[r], count(-1))
                    wait(pe, bank_free, value)
                    for j in range(J):
                        last = nc.tensor.transpose(pT_bank[r][:, j * N:(j + 1) * N], prob[b][:, r, j], ident[:])
                    last.then_inc(pT_made[r], 1)

                A, B, CC, NEXT = present(t, 0), present(t, -1), present(t, -2), present(t, 1)
                if B:
                    mask_scores()
                    wait(pe, q_done, count(0))
                    wait(pe, k_done, count(0))
                    for s in range(S):
                        scores(s, 0)
                        if s == 0:
                            wait(pe, x1T_lo_done, count(0))
                        last = matmul_split(v1_bank[:, s * D:(s + 1) * D],
                                            [(lambda c: x1T_hi[:, c, s], lambda c: wv1_hi[:, c]),
                                             (lambda c: x1T_hi[:, c, s], lambda c: wv1_lo[:, c]),
                                             (lambda c: x1T_lo[:, c, s], lambda c: wv1_hi[:, c])])
                        if s == S - 1:
                            last.then_inc(v1_made, 1)
                        last = scores(s, 1)
                    last.then_inc(scores_made, 1)
                if A:
                    wait(pe, u_hi_done, count(1))
                    wait(pe, o_done, count(-2))
                    if not present(t, -3):
                        wait(pe, xT_lo_done, count(1))
                    for s in range(S):
                        if s == 1:
                            wait(pe, q_done, count(0))
                        last = matmul_split(vr_bank[s][:, 0:D + N],
                                            [(lambda c: xT_hi[:, c, s], lambda c: wu_hi[:, c, s]),
                                             (lambda c: xT_lo[:, c, s], lambda c: wu_hi[:, c, s]),
                                             (lambda c: xT_hi[:, c, s], lambda c: wu_lo[:, c, s])],
                                            lambda: wait(pe, u_lo_done, count(1)) if s == 0 else None)
                        last.then_inc(vr_made[s], 1)
                if A:
                    for s in range(S):
                        wait(pe, relm_done[s], count(1))
                        last = nc.tensor.transpose(rt_bank[:, s * N:(s + 1) * N], relm[:, s], ident[:])
                    last.then_inc(rel_made, 1)
                    wait(pe, v1_done, count(0))
                    for s in range(S):
                        wait(pe, v0_done[s], count(1))
                        last = nc.tensor.matmul(o0_bank[:, s * D:(s + 1) * D], relm[:, s], v0_sb[:, s],
                                                start=True, stop=True)
                    last.then_inc(o0_made, 1)
                if CC:
                    if A:
                        transpose_probs(0, v0_done[0], count(1))
                        transpose_probs(1, v0_done[1], count(1))
                        transpose_probs(2, ssq_done, count(1))
                        transpose_probs(3, y0_done, count(1))
                    else:
                        transpose_probs(0, o_done, count(-2))
                        transpose_probs(1, oT_lo_done, count(-2))
                        transpose_probs(2, k_done, count(0))
                        transpose_probs(3, v1_done, count(0))
                if NEXT:
                    wait(pe, x_loaded[1 - b], dma_count(pe, t, 1, 1 - b))
                    if CC:
                        wait(pe, pT_done[0], count(-1))
                    transpose_x(x_sb[1 - b], xT_bank, xT_made)
                if CC:
                    for r in range(R):
                        wait(pe, pT_done[r], count(-1))
                    for s in range(S):
                        for c in range(C):
                            j = s * C + c
                            for r in range(R):
                                h = c * R + r
                                last = nc.tensor.matmul(ot_bank[HD * r:HD * (r + 1), j * N:(j + 1) * N],
                                                        v1[b][:, s, h * HD:(h + 1) * HD], pT[:, r, j],
                                                        start=True, stop=True)
                    last.then_inc(oT_made, 1)
                if NEXT:
                    if not CC:
                        wait(pe, ssq_done, count(1))
                    project_u(count)
                if A:
                    wait(pe, x1_done, count(1))
                    transpose_x(x1[b], x1T_bank, x1T_made)
                if CC:
                    wait(pe, oT_hi_done, count(-1))
                    if NEXT:
                        wait(pe, xT_lo_done, count(2))
                    for s in range(S):
                        last = matmul_split(pr_bank[:, s * D:(s + 1) * D],
                                            [(lambda c: oT_hi[:, s, c], lambda c: wp_hi[:, c]),
                                             (lambda c: oT_hi[:, s, c], lambda c: wp_lo[:, c]),
                                             (lambda c: oT_lo[:, s, c], lambda c: wp_hi[:, c])],
                                            lambda: wait(pe, oT_lo_done, count(-1)) if s == 0 else None)
                    last.then_inc(pr_made, 1)
                if A:
                    wait(pe, x1T_hi_done, count(1))
                    for part, bank, made in ((0, q_bank, q_made), (1, k_bank, k_made)):
                        if part == 0:
                            wait(pe, oT_lo_done, count(-1))
                        else:
                            wait(pe, u_lo_done, count(2))
                        for u in range(C):
                            last = weights_times(bank[:, u * S * N:(u + 1) * S * N], wqk_hi, wqk_lo,
                                                 part * D + u * 128, x1T_hi, x1T_lo,
                                                 lambda: wait(pe, x1T_lo_done, count(1)) if part + u == 0 else None)
                        last.then_inc(made, 1)
            run_steps(pe, step)


_INS = ['x', 'adj', 'L0_gnn_Wq', 'L0_gnn_Wk', 'L0_gnn_Wv', 'L1_gnn_w_qkv', 'L1_gnn_w_proj',
        'L1_gnn_b_proj', 'L1_gnn_ln_gamma', 'L1_gnn_ln_beta']
_OUTS = [((64, 128, 256), 'float32')]


def kernel(**inputs):
    import numpy as _np
    import concourse.bacc as _bacc
    from concourse import mybir as _mybir
    from concourse.bass_utils import run_bass_kernel_spmd as _run

    nc = _bacc.Bacc("TRN2", target_bir_lowering=False, num_devices=1)
    arrays, args = {}, []
    for name in _INS:
        a = _np.ascontiguousarray(inputs[name])
        arrays[f"in_{name}_dram"] = a
        args.append(nc.dram_tensor(f"in_{name}_dram", a.shape, _mybir.dt.from_np(a.dtype), kind="ExternalInput").ap())
    for i, (shape, dtype) in enumerate(_OUTS):
        dt = _mybir.dt.from_np(_np.dtype(dtype))
        args.append(nc.dram_tensor(f"out_{i}_dram", shape, dt, kind="ExternalOutput").ap())
    gnn_two_layer_kernel(nc, *args)
    r = _run(nc, [arrays], core_ids=[0])
    got = tuple(r.results[0][f"out_{i}_dram"] for i in range(len(_OUTS)))
    return got[0]
```

```python
import concourse.bass as bass
from concourse import mybir
from contextlib import ExitStack


def gnn_two_layer_kernel(nc, x, adj, wq0, wk0, wv0, w_qkv, w_proj, b_proj, gamma, beta, out):
    fp32 = mybir.dt.float32
    f32r = mybir.dt.float32r
    ALU = mybir.AluOpType
    ACT = mybir.ActivationFunctionType

    BATCH, N, D = x.shape
    H = 8
    HD = D // H
    S = 2
    C = D // 128
    R = 128 // HD
    J = S * C
    PAIRS = BATCH // S
    EPS = 1e-5
    SCALE = float(HD) ** -0.5
    MASKED = 1e30
    LARGEST = 3e38
    LOOP_FROM, LOOP_TO = 6, PAIRS - 2
    DMA = 16
    VECTOR_LOADS = 1 + 2 * S

    x_pairs = x.rearrange("(p s) n d -> p n s d", s=S)
    out_pairs = out.rearrange("(p s) n d -> p n s d", s=S)

    ctx = ExitStack()
    with ctx:
        def sb(name, shape, dt=fp32):
            return ctx.enter_context(nc.sbuf_tensor(name, shape, dt))

        def sem(name):
            return ctx.enter_context(nc.semaphore(name))

        wq0_sb = sb("wq0_sb", [128, C, D])
        wk0_sb = sb("wk0_sb", [128, C, D])
        wv0_sb = sb("wv0_sb", [128, C, D])
        wqkv_sb = sb("wqkv_sb", [128, C, 3 * D])
        wproj_sb = sb("wproj_sb", [128, C, D])
        adj_sb = sb("adj_sb", [N, N])
        bias2 = sb("bias2", [128, S, D])
        gamma_bc = sb("gamma_bc", [128, D])
        beta2 = sb("beta2", [128, S, D])
        ident = sb("ident", [128, 128])
        mask_sb = sb("mask_sb", [N, N])
        eps_c = sb("eps_c", [128, S])
        mhalf_c = sb("mhalf_c", [128, S])
        m_hi = sb("m_hi", [128, C, D], f32r)
        m_lo = sb("m_lo", [128, C, D], f32r)
        wu_hi = sb("wu_hi", [128, C, S, D + N], f32r)
        wu_lo = sb("wu_lo", [128, C, S, D + N], f32r)
        wqk_hi = sb("wqk_hi", [128, C, 2 * D], f32r)
        wqk_lo = sb("wqk_lo", [128, C, 2 * D], f32r)
        wv1_hi = sb("wv1_hi", [128, C, D], f32r)
        wv1_lo = sb("wv1_lo", [128, C, D], f32r)
        wp_hi = sb("wp_hi", [128, C, D], f32r)
        wp_lo = sb("wp_lo", [128, C, D], f32r)

        x_sb = [sb(f"x_sb{b}", [N, S, D]) for b in range(2)]
        xT_hi = sb("xT_hi", [128, C, S, N], f32r)
        xT_lo = sb("xT_lo", [128, C, S, N], f32r)
        v0_hi = sb("v0_hi", [N, S, D], f32r)
        v0_lo = sb("v0_lo", [N, S, D], f32r)
        relm = sb("relm", [N, S, N])
        relm_hi = sb("relm_hi", [N, S, N], f32r)
        relm_lo = sb("relm_lo", [N, S, N], f32r)
        sq_junk = sb("sq_junk", [N, S, N])
        ssq = sb("ssq", [N, S])
        rnorm = sb("rnorm", [N, S])
        y0 = sb("y0", [N, S, D])
        st0 = sb("st0", [N, S, 6])
        mv0 = sb("mv0", [N, S, 2])
        ve0 = sb("ve0", [N, S])
        rstd0 = sb("rstd0", [N, S])
        x1 = [sb(f"x1_{b}", [N, S, D]) for b in range(2)]
        x1b = [sb(f"x1b_{b}", [N, S, D]) for b in range(2)]
        x1T_hi = sb("x1T_hi", [128, C, S, N], f32r)
        x1T_lo = sb("x1T_lo", [128, C, S, N], f32r)
        qT = sb("qT", [128, C, S, N])
        kT = sb("kT", [128, C, S, N])
        v1 = [sb(f"v1_{b}", [N, S, D]) for b in range(2)]
        nmax = sb("nmax", [N, R, J])
        rsum = sb("rsum", [N, R, J])
        rinv = sb("rinv", [N, R, J])
        prob = [sb(f"prob{b}", [N, R, J, N]) for b in range(2)]
        pT = sb("pT", [N, R, J, N])
        oT_hi = sb("oT_hi", [128, S, C, N], f32r)
        oT_lo = sb("oT_lo", [128, S, C, N], f32r)
        o_sb = sb("o_sb", [N, S, D])
        ores = sb("ores", [N, S, D])
        og = sb("og", [N, S, D])
        y1 = sb("y1", [N, S, D])
        st1 = sb("st1", [N, S, 6])
        mv1 = sb("mv1", [N, S, 2])
        ve1 = sb("ve1", [N, S])
        rstd1 = sb("rstd1", [N, S])
        st2 = sb("st2", [N, S, 6])
        mv2 = sb("mv2", [N, S, 2])
        ve2 = sb("ve2", [N, S])
        rstd2 = sb("rstd2", [N, S])
        x2 = [sb(f"x2_{b}", [N, S, D]) for b in range(2)]

        score = [ctx.enter_context(nc.psum_tensor(f"score{r}", [128, J, N], fp32)) for r in range(R)]
        work = [ctx.enter_context(nc.psum_tensor(f"work{b}", [128, 512], fp32)) for b in range(4)]
        vr_bank, v1_bank, rt_bank = [work[0], work[1]], work[2], work[3]
        xT_bank, o0_bank, pT_bank = work[1], work[0], [work[3], work[2], work[1], work[3]]
        u_bank, ot_bank, x1T_bank, pr_bank = work[2], work[3], work[0], work[1]
        q_bank, k_bank = work[3], work[2]
        m_bank, wvT_bank = work[0], work[3]

        wqk0_loaded = sem("wqk0_loaded")
        wv0_loaded = sem("wv0_loaded")
        adj_loaded = sem("adj_loaded")
        wqkv_loaded = sem("wqkv_loaded")
        wproj_loaded = sem("wproj_loaded")
        vectors_loaded = sem("vectors_loaded")
        ident_zeroed = sem("ident_zeroed")
        ident_ready = sem("ident_ready")
        pool_consts = sem("pool_consts")
        mask_made = sem("mask_made")
        m_made = sem("m_made")
        m_hi_done = sem("m_hi_done")
        m_lo_done = sem("m_lo_done")
        wvT_made = sem("wvT_made")
        wvT_hi_done = sem("wvT_hi_done")
        wvT_lo_done = sem("wvT_lo_done")
        wq_scaled = sem("wq_scaled")
        wqk_hi_done = sem("wqk_hi_done")
        wqk_lo_done = sem("wqk_lo_done")
        wv1_hi_done = sem("wv1_hi_done")
        wv1_lo_done = sem("wv1_lo_done")
        wp_hi_done = sem("wp_hi_done")
        wp_lo_done = sem("wp_lo_done")
        x_loaded = [sem(f"x_loaded{b}") for b in range(2)]
        x2_stored = [sem(f"x2_stored{b}") for b in range(2)]
        xT_made = sem("xT_made")
        u_made = sem("u_made")
        vr_made = [sem(f"vr_made{s}") for s in range(S)]
        rel_made = sem("rel_made")
        o0_made = sem("o0_made")
        x1T_made = sem("x1T_made")
        q_made = sem("q_made")
        k_made = sem("k_made")
        v1_made = sem("v1_made")
        scores_made = sem("scores_made")
        pT_made = [sem(f"pT_made{r}") for r in range(R)]
        oT_made = sem("oT_made")
        pr_made = sem("pr_made")
        xT_hi_done = sem("xT_hi_done")
        u_hi_done = sem("u_hi_done")
        v0_hi_done = [sem(f"v0_hi_done{s}") for s in range(S)]
        relm_hi_done = sem("relm_hi_done")
        ssq_done = sem("ssq_done")
        x1T_hi_done = sem("x1T_hi_done")
        q_done = sem("q_done")
        k_done = sem("k_done")
        v1_done = sem("v1_done")
        exp_done = [sem(f"exp_done{r}") for r in range(R)]
        pT_done = [sem(f"pT_done{r}") for r in range(R)]
        oT_hi_done = sem("oT_hi_done")
        xT_lo_done = sem("xT_lo_done")
        u_lo_done = sem("u_lo_done")
        relm_done = [sem(f"relm_done{s}") for s in range(S)]
        v0_lo_done = [sem(f"v0_lo_done{s}") for s in range(S)]
        relm_lo_done = sem("relm_lo_done")
        y0_done = sem("y0_done")
        st0_done = sem("st0_done")
        mv0_done = sem("mv0_done")
        x1_done = sem("x1_done")
        x1T_lo_done = sem("x1T_lo_done")
        max_done = [sem(f"max_done{r}") for r in range(R)]
        rinv_done = [sem(f"rinv_done{r}") for r in range(R)]
        oT_lo_done = sem("oT_lo_done")
        o_done = sem("o_done")
        st1_done = sem("st1_done")
        mv1_done = sem("mv1_done")
        og_done = sem("og_done")
        y1_done = sem("y1_done")
        st2_done = sem("st2_done")
        mv2_done = sem("mv2_done")
        x2_done = sem("x2_done")
        rnorm_done = sem("rnorm_done")
        ve0_done = sem("ve0_done")
        rstd0_done = sem("rstd0_done")
        x1b_done = sem("x1b_done")
        prob_done = [sem(f"prob_done{r}") for r in range(R)]
        ores_done = sem("ores_done")
        ve1_done = sem("ve1_done")
        rstd1_done = sem("rstd1_done")
        ve2_done = sem("ve2_done")
        rstd2_done = sem("rstd2_done")

        def wait(eng, semaphore, count):
            if not (isinstance(count, int) and count <= 0):
                eng.wait_ge(semaphore, count)

        def counts(eng, t):
            kept = {}

            def count(c):
                if isinstance(t, int):
                    return min(t + c, PAIRS)
                if c not in kept:
                    kept[c] = eng.snap(t + c)
                return kept[c]
            return count

        def dma_count(eng, t, c, b):
            if isinstance(t, int):
                return DMA // 2 * (t + c - b) + DMA
            return eng.snap(DMA // 2 * t + (DMA // 2 * (c - b) + DMA))

        def run_steps(eng, step):
            for t in range(LOOP_FROM):
                step(t, t % 2)
            with eng.Fori(LOOP_FROM, LOOP_TO - 1, 2) as t:
                step(t, 0)
                step(t + 1, 1)
            for t in range(LOOP_TO, PAIRS + 3):
                step(t, t % 2)

        def present(t, c):
            return not isinstance(t, int) or 0 <= t + c < PAIRS

        def first(t, c):
            return isinstance(t, int) and t == c

        block = ctx.enter_context(nc.Block())

        @block.sync
        def _(sp):
            def chunks(w):
                return w.rearrange("(c p) n -> p c n", p=128)

            def on_all_rows(v):
                return v.rearrange("(a n) -> a n", a=1).to_broadcast([128, D])

            sp.dma_start(x_sb[0][:], x_pairs[0]).then_inc(x_loaded[0], DMA)
            sp.dma_start(wq0_sb[:], chunks(wq0)).then_inc(wqk0_loaded, DMA)
            sp.dma_start(wk0_sb[:], chunks(wk0)).then_inc(wqk0_loaded, DMA)
            sp.dma_start(wv0_sb[:], chunks(wv0)).then_inc(wv0_loaded, DMA)
            sp.dma_start(adj_sb[:], adj).then_inc(adj_loaded, DMA)
            sp.dma_start(wqkv_sb[:], chunks(w_qkv)).then_inc(wqkv_loaded, DMA)
            sp.dma_start(x_sb[1][:], x_pairs[1]).then_inc(x_loaded[1], DMA)
            sp.dma_start(wproj_sb[:], chunks(w_proj)).then_inc(wproj_loaded, DMA)
            sp.dma_start(gamma_bc[:], on_all_rows(gamma)).then_inc(vectors_loaded, DMA)
            for s in range(S):
                sp.dma_start(bias2[:, s], on_all_rows(b_proj)).then_inc(vectors_loaded, DMA)
                sp.dma_start(beta2[:, s], on_all_rows(beta)).then_inc(vectors_loaded, DMA)

            def step(t, b):
                count = counts(sp, t)
                if present(t, 2):
                    wait(sp, y0_done, count(1))
                    sp.dma_start(x_sb[b][:], x_pairs[t + 2]).then_inc(x_loaded[b], DMA)
                if present(t, -3):
                    wait(sp, x2_done, count(-2))
                    sp.dma_start(out_pairs[t - 3], x2[1 - b][:]).then_inc(x2_stored[1 - b], DMA)
            run_steps(sp, step)
            for b in range(2):
                sp.wait_ge(x2_stored[b], DMA * PAIRS // 2)

        @block.gpsimd
        def _(pool):
            nc.gpsimd.memset(ident[:], 0.0).then_inc(ident_zeroed, 1)
            nc.gpsimd.memset(eps_c[:], EPS).then_inc(pool_consts, 1)
            nc.gpsimd.memset(mhalf_c[:], -0.5).then_inc(pool_consts, 1)
            pool.wait_ge(ident_zeroed, 1)
            nc.gpsimd.affine_select(out=ident[:], in_=ident[:], compare_op=ALU.not_equal, fill=1.0, base=0,
                                    pattern=[[-1, 128]], channel_multiplier=1).then_inc(ident_ready, 1)
            pool.wait_ge(wqkv_loaded, DMA)
            nc.gpsimd.tensor_scalar(wqkv_sb[:, :, 0:D], wqkv_sb[:, :, 0:D], -SCALE, None, ALU.mult).then_inc(wq_scaled, 1)
            pool.wait_ge(pool_consts, 2)

            def inv_sqrt(mv, ve, ve_done, rstd, rstd_done, mv_ready, value):
                wait(pool, mv_ready, value)
                nc.gpsimd.tensor_tensor(ve[:], mv[:, :, 1], eps_c[:], ALU.add).then_inc(ve_done, 1)
                wait(pool, ve_done, value)
                nc.gpsimd.tensor_tensor(rstd[:], ve[:], mhalf_c[:], ALU.pow).then_inc(rstd_done, 1)

            def step(t, b):
                count = counts(pool, t)
                A, B, CC = present(t, 0), present(t, -1), present(t, -2)

                def normalise(r, c):
                    p = prob[(1 - b) if c == 0 else b]
                    wait(pool, rinv_done[r], count(c))
                    nc.gpsimd.tensor_tensor(p[:, r], p[:, r], rinv[:, r].unsqueeze(2).to_broadcast([N, J, N]),
                                            ALU.mult).then_inc(prob_done[r], 1)
                if CC:
                    normalise(R - 1, -1)
                if present(t, -3):
                    inv_sqrt(mv2, ve2, ve2_done, rstd2, rstd2_done, mv2_done, count(-2))
                if A:
                    wait(pool, ssq_done, count(1))
                    nc.gpsimd.tensor_tensor(rnorm[:], ssq[:], mhalf_c[:], ALU.pow).then_inc(rnorm_done, 1)
                    inv_sqrt(mv0, ve0, ve0_done, rstd0, rstd0_done, mv0_done, count(1))
                if B:
                    wait(pool, x1_done, count(0))
                    wait(pool, ores_done, count(-2))
                    if first(t, 1):
                        pool.wait_ge(vectors_loaded, VECTOR_LOADS * DMA)
                    nc.gpsimd.tensor_tensor(x1b[1 - b][:], x1[1 - b][:], beta2[:], ALU.add).then_inc(x1b_done, 1)
                    normalise(0, 0)
                    normalise(1, 0)
                if CC:
                    wait(pool, o_done, count(-1))
                    nc.gpsimd.tensor_tensor(ores[:], o_sb[:], x1b[b][:], ALU.add).then_inc(ores_done, 1)
                    inv_sqrt(mv1, ve1, ve1_done, rstd1, rstd1_done, mv1_done, count(-1))
                if B:
                    normalise(2, 0)
            run_steps(pool, step)

        @block.scalar
        def _(act):
            def split_hi(hi, full, done):
                nc.scalar.copy(hi, full).then_inc(done, 1)

            def copy_xT(count):
                wait(act, xT_made, count(2))
                nc.scalar.copy(xT_hi[:].rearrange("p c s n -> p (c s n)"), xT_bank[:]).then_inc(xT_hi_done, 1)

            def copy_u(count):
                wait(act, u_made, count(2))
                nc.scalar.copy(wu_hi[:, :, :, D:D + N],
                               u_bank[:].rearrange("p (c s n) -> p c s n", c=C, s=S)).then_inc(u_hi_done, 1)

            def step(t, b):
                count = counts(act, t)
                A, B, CC, NEXT = present(t, 0), present(t, -1), present(t, -2), present(t, 1)

                def copy_v0(s):
                    wait(act, relm_done[s], count(1))
                    wait(act, o0_made, count(0))
                    nc.scalar.copy(v0_hi[:, s], vr_bank[s][:, 0:D]).then_inc(v0_hi_done[s], 1)

                def copy_pT(r):
                    wait(act, pT_made[r], count(-1))
                    wait(act, oT_made, count(-2))
                    nc.scalar.copy(pT[:, r].rearrange("p j n -> p (j n)"), pT_bank[r][:]).then_inc(pT_done[r], 1)

                def exps(r):
                    wait(act, max_done[r], count(0))
                    wait(act, pT_made[r], count(-2))
                    for j in range(J):
                        last = nc.scalar.activation(prob[1 - b][:, r, j], score[r][:, j], ACT.Exp,
                                                    bias=nmax[:, r, j:j + 1], scale=-1.0,
                                                    accum_out=rsum[:, r, j:j + 1])
                    last.then_inc(exp_done[r], 1)

                if A:
                    copy_v0(0)
                    copy_v0(1)
                    nc.scalar.copy(relm_hi[:], relm[:]).then_inc(relm_hi_done, 1)
                if B:
                    wait(act, v1_made, count(0))
                    wait(act, oT_made, count(-2))
                    nc.scalar.copy(v1[1 - b][:].rearrange("p s n -> p (s n)"), v1_bank[:]).then_inc(v1_done, 1)
                if A:
                    wait(act, rel_made, count(1))
                    for s in range(S):
                        last = nc.scalar.activation(sq_junk[:, s], rt_bank[:, s * N:(s + 1) * N], ACT.Square,
                                                    accum_out=ssq[:, s:s + 1])
                    last.then_inc(ssq_done, 1)
                    if first(t, 0):
                        act.wait_ge(wqkv_loaded, DMA)
                        split_hi(wv1_hi[:], wqkv_sb[:, :, 2 * D:3 * D], wv1_hi_done)
                    if first(t, 1):
                        act.wait_ge(wproj_loaded, DMA)
                        split_hi(wp_hi[:], wproj_sb[:], wp_hi_done)
                if NEXT:
                    copy_xT(count)
                if CC:
                    for r in range(R):
                        copy_pT(r)
                if B:
                    exps(0)
                if CC:
                    wait(act, oT_made, count(-1))
                    wait(act, pr_made, count(-2))
                    nc.scalar.copy(oT_hi[:].rearrange("p s c n -> p (s c n)"), ot_bank[:]).then_inc(oT_hi_done, 1)
                if NEXT:
                    copy_u(count)
                if A:
                    wait(act, x1T_made, count(1))
                    nc.scalar.copy(x1T_hi[:].rearrange("p c s n -> p (c s n)"), x1T_bank[:]).then_inc(x1T_hi_done, 1)
                if B:
                    exps(1)
                    exps(2)
                if A:
                    wait(act, q_made, count(1))
                    nc.scalar.copy(qT[:].rearrange("p c s n -> p (c s n)"), q_bank[:]).then_inc(q_done, 1)
                    wait(act, k_made, count(1))
                    nc.scalar.copy(kT[:].rearrange("p c s n -> p (c s n)"), k_bank[:]).then_inc(k_done, 1)
                if B:
                    exps(3)
            copy_xT(lambda c: 1)
            act.wait_ge(m_made, 1)
            split_hi(m_hi[:], m_bank[:].rearrange("p (c n) -> p c n", c=C), m_hi_done)
            act.wait_ge(wvT_made, 1)
            for s in range(S):
                split_hi(wu_hi[:, :, s, 0:D], wvT_bank[:].rearrange("p (c n) -> p c n", c=C), wvT_hi_done)
            copy_u(lambda c: 1)
            act.wait_ge(wq_scaled, 1)
            split_hi(wqk_hi[:], wqkv_sb[:, :, 0:2 * D], wqk_hi_done)
            run_steps(act, step)

        @block.vector
        def _(dve):
            def split_lo(lo, full, hi, hi_done, done, value=1):
                dve.wait_ge(hi_done, value)
                nc.vector.tensor_tensor(lo, full, hi.bitcast(fp32), ALU.subtract).then_inc(done, 1)

            def split_xT(value):
                wait(dve, xT_hi_done, value)
                nc.vector.tensor_tensor(xT_lo[:].rearrange("p c s n -> p (c s n)"), xT_bank[:],
                                        xT_hi[:].bitcast(fp32).rearrange("p c s n -> p (c s n)"),
                                        ALU.subtract).then_inc(xT_lo_done, 1)

            def split_u(value):
                wait(dve, u_hi_done, value)
                nc.vector.tensor_tensor(wu_lo[:, :, :, D:D + N],
                                        u_bank[:].rearrange("p (c s n) -> p c s n", c=C, s=S),
                                        wu_hi[:, :, :, D:D + N].bitcast(fp32), ALU.subtract).then_inc(u_lo_done, 1)

            split_xT(1)
            split_lo(m_lo[:], m_bank[:].rearrange("p (c n) -> p c n", c=C), m_hi[:], m_hi_done, m_lo_done)
            for s in range(S):
                split_lo(wu_lo[:, :, s, 0:D], wvT_bank[:].rearrange("p (c n) -> p c n", c=C), wu_hi[:, :, s, 0:D],
                         wvT_hi_done, wvT_lo_done, S)
            dve.wait_ge(adj_loaded, DMA)
            nc.vector.tensor_scalar(mask_sb[:], adj_sb[:], 0.0, MASKED, ALU.is_equal, ALU.mult).then_inc(mask_made, 1)
            split_u(1)

            def step(t, b):
                count = counts(dve, t)

                def norm_stats(y, st, mv, st_done, mv_done, value):
                    for s in range(S):
                        last = nc.vector.bn_stats(st[:, s], y[:, s])
                    last.then_inc(st_done, 1)
                    dve.wait_ge(mask_made, 1)
                    wait(dve, st_done, value)
                    for s in range(S):
                        last = nc.vector.bn_aggr(mv[:, s], st[:, s])
                    last.then_inc(mv_done, 1)

                def maxes(r, first_j=0, end_j=J):
                    dve.wait_ge(mask_made, 1)
                    if r == 0:
                        wait(dve, scores_made, count(0))
                    for j in range(first_j, end_j):
                        last = nc.vector.tensor_tensor_reduce(out=score[r][:, j], in0=score[r][:, j], in1=mask_sb[:],
                                                              scale=1.0, scalar=LARGEST, op0=ALU.add, op1=ALU.min,
                                                              accum_out=nmax[:, r, j:j + 1])
                    if end_j == J:
                        last.then_inc(max_done[r], 1)

                def inverses(r, c):
                    wait(dve, exp_done[r], count(c))
                    wait(dve, prob_done[r], count(c - 1))
                    nc.vector.reciprocal(rinv[:, r], rsum[:, r]).then_inc(rinv_done[r], 1)

                def mask_rel(s):
                    wait(dve, vr_made[s], count(1))
                    nc.vector.tensor_tensor(relm[:, s], vr_bank[s][:, D:D + N], adj_sb[:],
                                            ALU.mult).then_inc(relm_done[s], 1)

                A, B, CC, NEXT = present(t, 0), present(t, -1), present(t, -2), present(t, 1)
                LAST = present(t, -3)
                if A:
                    mask_rel(0)
                    mask_rel(1)
                if CC:
                    inverses(R - 1, -1)
                if A:
                    for s in range(S):
                        wait(dve, v0_hi_done[s], count(1))
                        nc.vector.tensor_tensor(v0_lo[:, s], vr_bank[s][:, 0:D], v0_hi[:, s].bitcast(fp32),
                                                ALU.subtract).then_inc(v0_lo_done[s], 1)
                    wait(dve, relm_hi_done, count(1))
                    nc.vector.tensor_tensor(relm_lo[:], relm[:], relm_hi[:].bitcast(fp32),
                                            ALU.subtract).then_inc(relm_lo_done, 1)
                if LAST:
                    wait(dve, og_done, count(-2))
                    wait(dve, rstd1_done, count(-2))
                    wait(dve, ores_done, count(-2))
                    wait(dve, x2_done, count(-3))
                    for s in range(S):
                        last = nc.vector.scalar_tensor_tensor(y1[:, s], og[:, s], rstd1[:, s:s + 1], ores[:, s],
                                                              ALU.mult, ALU.add)
                    last.then_inc(y1_done, 1)
                    wait(dve, y1_done, count(-2))
                    norm_stats(y1, st2, mv2, st2_done, mv2_done, count(-2))
                if NEXT:
                    split_xT(count(2))
                if B:
                    maxes(0)
                if A:
                    wait(dve, o0_made, count(1))
                    wait(dve, rnorm_done, count(1))
                    for s in range(S):
                        last = nc.vector.scalar_tensor_tensor(y0[:, s], o0_bank[:, s * D:(s + 1) * D], rnorm[:, s:s + 1],
                                                              x_sb[b][:, s], ALU.mult, ALU.add)
                    last.then_inc(y0_done, 1)
                    wait(dve, y0_done, count(1))
                    norm_stats(y0, st0, mv0, st0_done, mv0_done, count(1))
                if B:
                    maxes(1)
                    if not A:
                        maxes(2)
                        maxes(3)
                if A:
                    wait(dve, rstd0_done, count(1))
                    wait(dve, x1b_done, count(-1))
                    for s in range(S):
                        last = nc.vector.tensor_scalar(x1[b][:, s], y0[:, s], mv0[:, s, 0:1], rstd0[:, s:s + 1],
                                                       ALU.subtract, ALU.mult)
                    last.then_inc(x1_done, 1)
                    if first(t, 0):
                        split_lo(wqk_lo[:], wqkv_sb[:, :, 0:2 * D], wqk_hi[:], wqk_hi_done, wqk_lo_done)
                if A and B:
                    maxes(2, 0, J // 2)
                if CC:
                    wait(dve, oT_hi_done, count(-1))
                    nc.vector.tensor_tensor(oT_lo[:].rearrange("p s c n -> p (s c n)"), ot_bank[:],
                                            oT_hi[:].bitcast(fp32).rearrange("p s c n -> p (s c n)"),
                                            ALU.subtract).then_inc(oT_lo_done, 1)
                if B:
                    inverses(0, 0)
                    if A:
                        maxes(2, J // 2, J)
                if A:
                    wait(dve, x1T_hi_done, count(1))
                    nc.vector.tensor_tensor(x1T_lo[:].rearrange("p c s n -> p (c s n)"), x1T_bank[:],
                                            x1T_hi[:].bitcast(fp32).rearrange("p c s n -> p (c s n)"),
                                            ALU.subtract).then_inc(x1T_lo_done, 1)
                if NEXT:
                    split_u(count(2))
                if B:
                    if A:
                        maxes(3)
                    inverses(1, 0)
                if first(t, 1):
                    split_lo(wp_lo[:], wproj_sb[:], wp_hi[:], wp_hi_done, wp_lo_done)
                if first(t, 0):
                    split_lo(wv1_lo[:], wqkv_sb[:, :, 2 * D:3 * D], wv1_hi[:], wv1_hi_done, wv1_lo_done)
                if CC:
                    if first(t, 2):
                        dve.wait_ge(vectors_loaded, VECTOR_LOADS * DMA)
                    wait(dve, pr_made, count(-1))
                    wait(dve, ores_done, count(-2))
                    nc.vector.tensor_tensor(o_sb[:].rearrange("p s n -> p (s n)"), pr_bank[:],
                                            bias2[:].rearrange("p s n -> p (s n)"), ALU.add).then_inc(o_done, 1)
                    wait(dve, o_done, count(-1))
                    norm_stats(o_sb, st1, mv1, st1_done, mv1_done, count(-1))
                    wait(dve, mv1_done, count(-1))
                    for s in range(S):
                        last = nc.vector.scalar_tensor_tensor(og[:, s], o_sb[:, s], mv1[:, s, 0:1], gamma_bc[:],
                                                              ALU.subtract, ALU.mult)
                    last.then_inc(og_done, 1)
                if B:
                    inverses(2, 0)
                if LAST:
                    wait(dve, rstd2_done, count(-2))
                    wait(dve, x2_stored[1 - b], dma_count(dve, t, -5, 1 - b))
                    for s in range(S):
                        last = nc.vector.tensor_scalar(x2[1 - b][:, s], y1[:, s], mv2[:, s, 0:1], rstd2[:, s:s + 1],
                                                       ALU.subtract, ALU.mult)
                    last.then_inc(x2_done, 1)
            run_steps(dve, step)

        @block.tensor
        def _(pe):
            def matmul_split(bank, passes, before_last=None):
                for n, (l, r) in enumerate(passes):
                    if n == 2 and before_last is not None:
                        before_last()
                    for c in range(C):
                        last = nc.tensor.matmul(bank, l(c), r(c), start=(n == 0 and c == 0),
                                                stop=(n == 2 and c == C - 1))
                return last

            def weights_times(bank, w_hi, w_lo, at, a_hi, a_lo, before_last=None):
                def weights(w):
                    return lambda c: w[:, c, at:at + 128]

                def tokens(a):
                    return lambda c: a[:, c].rearrange("p s n -> p (s n)")
                return matmul_split(bank, [(weights(w_hi), tokens(a_hi)), (weights(w_lo), tokens(a_hi)),
                                           (weights(w_hi), tokens(a_lo))], before_last)

            def transpose_x(src, bank, made):
                for c in range(C):
                    for s in range(S):
                        last = nc.tensor.transpose(bank[:, (c * S + s) * N:(c * S + s + 1) * N],
                                                   src[:, s, c * 128:(c + 1) * 128], ident[:])
                last.then_inc(made, 1)

            def project_u(u, count):
                if u == 0:
                    wait(pe, xT_hi_done, count(2))
                last = weights_times(u_bank[:, u * S * N:(u + 1) * S * N], m_hi, m_lo, u * 128, xT_hi, xT_lo,
                                     lambda: wait(pe, xT_lo_done, count(2)) if u == 0 else None)
                if u == C - 1:
                    last.then_inc(u_made, 1)

            pe.wait_ge(ident_ready, 1)
            pe.wait_ge(x_loaded[0], DMA)
            transpose_x(x_sb[0], xT_bank, xT_made)
            pe.wait_ge(wqk0_loaded, 2 * DMA)
            for a in range(C):
                for e in range(C):
                    last = nc.tensor.matmul(m_bank[:, a * D:(a + 1) * D], wq0_sb[:, e, a * 128:(a + 1) * 128],
                                            wk0_sb[:, e, :], start=(e == 0), stop=(e == C - 1))
            last.then_inc(m_made, 1)
            pe.wait_ge(wv0_loaded, DMA)
            for c in range(C):
                for e in range(C):
                    last = nc.tensor.transpose(wvT_bank[:, c * D + e * 128:c * D + (e + 1) * 128],
                                               wv0_sb[:, e, c * 128:(c + 1) * 128], ident[:])
            last.then_inc(wvT_made, 1)
            pe.wait_ge(m_lo_done, 1)
            for u in range(C):
                project_u(u, lambda c: c - 1)
            pe.wait_ge(wvT_lo_done, S)

            def step(t, b):
                count = counts(pe, t)

                def scores(s, c):
                    j = s * C + c
                    for r in range(R):
                        if j == 0:
                            wait(pe, exp_done[r], count(-1))
                        last = nc.tensor.matmul(score[r][:, j], qT[HD * r:HD * (r + 1), c, s, :],
                                                kT[HD * r:HD * (r + 1), c, s, :], start=True, stop=True)
                    return last

                def transpose_probs(r):
                    wait(pe, prob_done[r], count(-1))
                    for j in range(J):
                        last = nc.tensor.transpose(pT_bank[r][:, j * N:(j + 1) * N], prob[b][:, r, j], ident[:])
                    last.then_inc(pT_made[r], 1)

                def values1(s):
                    last = matmul_split(v1_bank[:, s * D:(s + 1) * D],
                                        [(lambda c: x1T_hi[:, c, s], lambda c: wv1_hi[:, c]),
                                         (lambda c: x1T_hi[:, c, s], lambda c: wv1_lo[:, c]),
                                         (lambda c: x1T_lo[:, c, s], lambda c: wv1_hi[:, c])])
                    if s == S - 1:
                        last.then_inc(v1_made, 1)

                def values_rel(s):
                    if s == 0:
                        wait(pe, u_hi_done, count(1))
                    else:
                        wait(pe, o_done, count(-2))
                    last = matmul_split(vr_bank[s][:, 0:D + N],
                                        [(lambda c: xT_hi[:, c, s], lambda c: wu_hi[:, c, s]),
                                         (lambda c: xT_lo[:, c, s], lambda c: wu_hi[:, c, s]),
                                         (lambda c: xT_hi[:, c, s], lambda c: wu_lo[:, c, s])],
                                        lambda: wait(pe, u_lo_done, count(1)) if s == 0 else None)
                    last.then_inc(vr_made[s], 1)

                A, B, CC, NEXT = present(t, 0), present(t, -1), present(t, -2), present(t, 1)
                if A:
                    values_rel(0)
                    values_rel(1)
                if B:
                    if not A:
                        wait(pe, k_done, count(0))
                        values1(0)
                        values1(1)
                    wait(pe, q_done, count(0))
                    wait(pe, k_done, count(0))
                    scores(0, 0)
                    scores(0, 1)
                    if first(t, 1):
                        pe.wait_ge(wv1_lo_done, 1)
                    if A:
                        values1(0)
                        values1(1)
                    else:
                        transpose_probs(0)
                if A:
                    for s in range(S):
                        wait(pe, relm_done[s], count(1))
                        last = nc.tensor.transpose(rt_bank[:, s * N:(s + 1) * N], relm[:, s], ident[:])
                    last.then_inc(rel_made, 1)
                if NEXT:
                    wait(pe, x_loaded[1 - b], dma_count(pe, t, 1, 1 - b))
                    wait(pe, v0_lo_done[1], count(1))
                    transpose_x(x_sb[1 - b], xT_bank, xT_made)
                if B:
                    scores(1, 0)
                    scores(1, 1).then_inc(scores_made, 1)
                if A:
                    for s in range(S):
                        wait(pe, v0_lo_done[s], count(1))
                        if s == 0:
                            wait(pe, relm_lo_done, count(1))
                        for n, (rel, v) in enumerate(((relm_hi, v0_hi), (relm_lo, v0_hi), (relm_hi, v0_lo))):
                            last = nc.tensor.matmul(o0_bank[:, s * D:(s + 1) * D], rel[:, s], v[:, s],
                                                    start=(n == 0), stop=(n == 2))
                    last.then_inc(o0_made, 1)
                if CC:
                    wait(pe, ssq_done, count(1))
                    if A or not B:
                        transpose_probs(0)
                    wait(pe, v1_done, count(0))
                    transpose_probs(1)
                    wait(pe, xT_lo_done, count(2))
                    if not A:
                        wait(pe, o_done, count(-2))
                    transpose_probs(2)
                    wait(pe, pT_done[0], count(-1))
                    transpose_probs(3)
                if NEXT:
                    if CC:
                        wait(pe, pT_done[1], count(-1))
                    elif B:
                        wait(pe, v1_done, count(0))
                    project_u(0, count)
                if CC:
                    for r in range(R):
                        wait(pe, pT_done[r], count(-1))
                    for s in range(S):
                        for c in range(C):
                            j = s * C + c
                            for r in range(R):
                                h = c * R + r
                                last = nc.tensor.matmul(ot_bank[HD * r:HD * (r + 1), j * N:(j + 1) * N],
                                                        v1[b][:, s, h * HD:(h + 1) * HD], pT[:, r, j],
                                                        start=True, stop=True)
                    last.then_inc(oT_made, 1)
                if NEXT:
                    for u in range(1, C):
                        project_u(u, count)
                if A:
                    wait(pe, x1_done, count(1))
                    transpose_x(x1[b], x1T_bank, x1T_made)
                if CC:
                    wait(pe, oT_hi_done, count(-1))
                    if first(t, 2):
                        pe.wait_ge(wp_lo_done, 1)
                    for s in range(S):
                        last = matmul_split(pr_bank[:, s * D:(s + 1) * D],
                                            [(lambda c: oT_hi[:, s, c], lambda c: wp_hi[:, c]),
                                             (lambda c: oT_hi[:, s, c], lambda c: wp_lo[:, c]),
                                             (lambda c: oT_lo[:, s, c], lambda c: wp_hi[:, c])],
                                            lambda: wait(pe, oT_lo_done, count(-1)) if s == 0 else None)
                    last.then_inc(pr_made, 1)
                if A:
                    wait(pe, x1T_hi_done, count(1))
                    if first(t, 0):
                        pe.wait_ge(wqk_lo_done, 1)
                    for part, bank, made in ((0, q_bank, q_made), (1, k_bank, k_made)):
                        if part == 1:
                            wait(pe, u_lo_done, count(2))
                        for u in range(C):
                            last = weights_times(bank[:, u * S * N:(u + 1) * S * N], wqk_hi, wqk_lo,
                                                 part * D + u * 128, x1T_hi, x1T_lo,
                                                 lambda: wait(pe, x1T_lo_done, count(1)) if part + u == 0 else None)
                        last.then_inc(made, 1)
            run_steps(pe, step)


_INS = ['x', 'adj', 'L0_gnn_Wq', 'L0_gnn_Wk', 'L0_gnn_Wv', 'L1_gnn_w_qkv', 'L1_gnn_w_proj',
        'L1_gnn_b_proj', 'L1_gnn_ln_gamma', 'L1_gnn_ln_beta']
_OUTS = [((64, 128, 256), 'float32')]


def kernel(**inputs):
    import numpy as _np
    import concourse.bacc as _bacc
    from concourse import mybir as _mybir
    from concourse.bass_utils import run_bass_kernel_spmd as _run

    nc = _bacc.Bacc("TRN2", target_bir_lowering=False, num_devices=1)
    arrays, args = {}, []
    for name in _INS:
        a = _np.ascontiguousarray(inputs[name])
        arrays[f"in_{name}_dram"] = a
        args.append(nc.dram_tensor(f"in_{name}_dram", a.shape, _mybir.dt.from_np(a.dtype), kind="ExternalInput").ap())
    for i, (shape, dtype) in enumerate(_OUTS):
        dt = _mybir.dt.from_np(_np.dtype(dtype))
        args.append(nc.dram_tensor(f"out_{i}_dram", shape, dt, kind="ExternalOutput").ap())
    gnn_two_layer_kernel(nc, *args)
    r = _run(nc, [arrays], core_ids=[0])
    got = tuple(r.results[0][f"out_{i}_dram"] for i in range(len(_OUTS)))
    return got[0]
```
